# Optimizing a Trainium2 kernel written in Bass

```python
import numpy as np
import jax
import jax.numpy as jnp

def _softmax(x, axis=-1):
    return jax.nn.softmax(x, axis=axis)
def _gelu(x):
    return jax.nn.gelu(x, approximate=True)
def _silu(x):
    return jax.nn.silu(x)
def _sigmoid(x):
    return jax.nn.sigmoid(x)
def _layernorm(x, axis=-1, eps=1e-5):
    m = jnp.mean(x, axis=axis, keepdims=True)
    v = jnp.var(x, axis=axis, keepdims=True)
    return (x - m) / jnp.sqrt(v + eps)
def _scatter_add(tgt, idx, src, axis=0):
    return tgt.at[idx].add(src)
def _segment_sum(src, seg, n):
    return jax.ops.segment_sum(src, seg, n)

kernel_name = 'mk_conv_seq_d2_conv_nchw128_9f30ec'

def setup_inputs(seed: int = 0):
    np.random.seed(seed)
    _w = jnp.asarray
    def _rec_inputs():
        import jax
        import jax.numpy as jnp
        _gk = jax.random.key(seed)
        x = -0.0005207 + 1.001 * jax.random.normal(jax.random.fold_in(_gk, 1), (4, 128, 64, 64), jnp.float32)
        return x
    x = _rec_inputs()
    def _L0_conv_setup():
        import jax, jax.numpy as jnp
        import numpy as np
        C = 128
        NUM_GROUPS = 32
        EPS = 1e-06

        def group_norm(x, gamma, beta):
            N, Cc, H, W = x.shape
            xg = x.reshape(N, NUM_GROUPS, -1)
            mean = xg.mean(axis=-1, keepdims=True)
            var = ((xg - mean) ** 2).mean(axis=-1, keepdims=True)
            xn = ((xg - mean) * jax.lax.rsqrt(var + EPS)).reshape(N, Cc, H, W)
            return xn * gamma[None, :, None, None] + beta[None, :, None, None]

        def conv1x1(x, w, b):
            return jnp.einsum('nchw,oc->nohw', x, w) + b[None, :, None, None]
        key = jax.random.key(seed)
        ks = jax.random.split(key, 11)
        s = 1.0 / np.sqrt(C)
        return {'x': jax.random.normal(ks[0], (4, C, 64, 64), dtype=jnp.float32), 'gamma': jnp.ones((C,), jnp.float32), 'beta': jnp.zeros((C,), jnp.float32), 'wq': jax.random.normal(ks[1], (C, C), jnp.float32) * s, 'bq': jnp.zeros((C,), jnp.float32), 'wk': jax.random.normal(ks[2], (C, C), jnp.float32) * s, 'bk': jnp.zeros((C,), jnp.float32), 'wv': jax.random.normal(ks[3], (C, C), jnp.float32) * s, 'bv': jnp.zeros((C,), jnp.float32), 'wo': jax.random.normal(ks[4], (C, C), jnp.float32) * s, 'bo': jnp.zeros((C,), jnp.float32)}
    _L0_conv_all = _L0_conv_setup()
    _L0_conv_in = {k: v for k, v in _L0_conv_all.items() if k in ('gamma', 'beta', 'wq', 'bq', 'wk', 'bk', 'wv', 'bv', 'wo', 'bo', )}
    del _L0_conv_all

    def _L1_conv_setup():
        import jax, jax.numpy as jnp
        import numpy as np
        B, C, H, W = (8, 128, 64, 64)
        CI = C // 2
        key = jax.random.key(seed)
        ks = jax.random.split(key, 5)
        s_in = 1.0 / np.sqrt(C)
        s_ci = 1.0 / np.sqrt(CI)
        return {'x': jax.random.normal(ks[0], (B, C, H, W), dtype=jnp.float32), 'theta_w': jax.random.normal(ks[1], (CI, C), dtype=jnp.float32) * s_in, 'theta_b': jnp.zeros((CI,), dtype=jnp.float32), 'phi_w': jax.random.normal(ks[2], (CI, C), dtype=jnp.float32) * s_in, 'phi_b': jnp.zeros((CI,), dtype=jnp.float32), 'g_w': jax.random.normal(ks[3], (CI, C), dtype=jnp.float32) * s_in, 'g_b': jnp.zeros((CI,), dtype=jnp.float32), 'W_w': jax.random.normal(ks[4], (C, CI), dtype=jnp.float32) * s_ci, 'W_b': jnp.zeros((C,), dtype=jnp.float32)}
    _L1_conv_all = _L1_conv_setup()
    _L1_conv_in = {k: v for k, v in _L1_conv_all.items() if k in ('theta_w', 'theta_b', 'phi_w', 'phi_b', 'g_w', 'g_b', 'W_w', 'W_b', )}
    del _L1_conv_all

    return {
        "x": x,
        "L0_conv_gamma": _L0_conv_in["gamma"],
        "L0_conv_beta": _L0_conv_in["beta"],
        "L0_conv_wq": _L0_conv_in["wq"],
        "L0_conv_bq": _L0_conv_in["bq"],
        "L0_conv_wk": _L0_conv_in["wk"],
        "L0_conv_bk": _L0_conv_in["bk"],
        "L0_conv_wv": _L0_conv_in["wv"],
        "L0_conv_bv": _L0_conv_in["bv"],
        "L0_conv_wo": _L0_conv_in["wo"],
        "L0_conv_bo": _L0_conv_in["bo"],
        "L1_conv_theta_w": _L1_conv_in["theta_w"],
        "L1_conv_theta_b": _L1_conv_in["theta_b"],
        "L1_conv_phi_w": _L1_conv_in["phi_w"],
        "L1_conv_phi_b": _L1_conv_in["phi_b"],
        "L1_conv_g_w": _L1_conv_in["g_w"],
        "L1_conv_g_b": _L1_conv_in["g_b"],
        "L1_conv_W_w": _L1_conv_in["W_w"],
        "L1_conv_W_b": _L1_conv_in["W_b"],
    }

def reference(x, L0_conv_gamma, L0_conv_beta, L0_conv_wq, L0_conv_bq, L0_conv_wk, L0_conv_bk, L0_conv_wv, L0_conv_bv, L0_conv_wo, L0_conv_bo, L1_conv_theta_w, L1_conv_theta_b, L1_conv_phi_w, L1_conv_phi_b, L1_conv_g_w, L1_conv_g_b, L1_conv_W_w, L1_conv_W_b):
    import jax
    import jax.numpy as jnp
    def _L0_conv_ref(x, gamma, beta, wq, bq, wk, bk, wv, bv, wo, bo):
        import jax, jax.numpy as jnp
        import numpy as np
        C = 128
        NUM_GROUPS = 32
        EPS = 1e-06

        def group_norm(x, gamma, beta):
            N, Cc, H, W = x.shape
            xg = x.reshape(N, NUM_GROUPS, -1)
            mean = xg.mean(axis=-1, keepdims=True)
            var = ((xg - mean) ** 2).mean(axis=-1, keepdims=True)
            xn = ((xg - mean) * jax.lax.rsqrt(var + EPS)).reshape(N, Cc, H, W)
            return xn * gamma[None, :, None, None] + beta[None, :, None, None]

        def conv1x1(x, w, b):
            return jnp.einsum('nchw,oc->nohw', x, w) + b[None, :, None, None]
        N, Cc, H, W = x.shape
        L = H * W
        xn = group_norm(x, gamma, beta)
        q = conv1x1(xn, wq, bq).reshape(N, Cc, L)
        k = conv1x1(xn, wk, bk).reshape(N, Cc, L)
        v = conv1x1(xn, wv, bv).reshape(N, Cc, L)
        scale = 1.0 / jnp.sqrt(jnp.asarray(Cc, x.dtype))
        scores = jnp.einsum('ncl,ncm->nlm', q, k) * scale
        weights = jax.nn.softmax(scores, axis=-1)
        attn = jnp.einsum('nlm,ncm->ncl', weights, v).reshape(N, Cc, H, W)
        return x + conv1x1(attn, wo, bo)

    def _L1_conv_ref(x, theta_w, theta_b, phi_w, phi_b, g_w, g_b, W_w, W_b):
        import jax, jax.numpy as jnp
        import numpy as np
        B, C, H, W = (8, 128, 64, 64)
        CI = C // 2
        b, c, h, w = x.shape
        n = h * w
        xf = x.reshape(b, c, n)
        theta = jnp.einsum('oc,bcn->bon', theta_w, xf) + theta_b[:, None]
        phi = jnp.einsum('oc,bcn->bon', phi_w, xf) + phi_b[:, None]
        g = jnp.einsum('oc,bcn->bon', g_w, xf) + g_b[:, None]
        scores = jnp.einsum('bci,bcj->bij', theta, phi)
        attention = jax.nn.softmax(scores, axis=-1)
        out = jnp.einsum('bci,bij->bcj', g, attention)
        out = jnp.einsum('oc,bcn->bon', W_w, out) + W_b[:, None]
        return x + out.reshape(b, c, h, w)

    def _gn(v, G=32, eps=1e-5):
        B_, C_, H_, W_ = v.shape
        g = v.reshape(B_, G, C_ // G, H_, W_)
        m = jnp.mean(g, axis=(2, 3, 4), keepdims=True)
        s = jnp.var(g, axis=(2, 3, 4), keepdims=True)
        return ((g - m) / jnp.sqrt(s + eps)).reshape(v.shape)

    def _ln_c(v, eps=1e-6):
        m = jnp.mean(v, axis=1, keepdims=True)
        s = jnp.var(v, axis=1, keepdims=True)
        return (v - m) / jnp.sqrt(s + eps)

    def _ln_t(v, eps=1e-5):
        m = jnp.mean(v, axis=-1, keepdims=True)
        s = jnp.var(v, axis=-1, keepdims=True)
        return (v - m) / jnp.sqrt(s + eps)

    def _to_tokens(v):
        B_, C_, H_, W_ = v.shape
        return v.reshape(B_, C_, H_ * W_).transpose(0, 2, 1)
    def _from_tokens(t, like):
        B_, C_, H_, W_ = like.shape
        return t.transpose(0, 2, 1).reshape(B_, C_, H_, W_)

    x = _L0_conv_ref(x, L0_conv_gamma, L0_conv_beta, L0_conv_wq, L0_conv_bq, L0_conv_wk, L0_conv_bk, L0_conv_wv, L0_conv_bv, L0_conv_wo, L0_conv_bo)
    x = _L1_conv_ref(x, L1_conv_theta_w, L1_conv_theta_b, L1_conv_phi_w, L1_conv_phi_b, L1_conv_g_w, L1_conv_g_b, L1_conv_W_w, L1_conv_W_b)
    return x


_drawn_inputs = setup_inputs


def setup_inputs(seed=0):
    import zlib

    import numpy as np

    out = dict(_drawn_inputs(seed))
    spreads = {'L0_conv_gamma': (1.0, 0.2),
     'L0_conv_beta': (0.0, 0.1),
     'L0_conv_bq': (0.0, 0.345),
     'L0_conv_bk': (0.0, 0.8),
     'L0_conv_bv': (0.0, 0.1),
     'L0_conv_bo': (0.0, 0.1),
     'L1_conv_theta_b': (0.0, 0.1),
     'L1_conv_phi_b': (0.0, 0.8),
     'L1_conv_g_b': (0.0, 0.1),
     'L1_conv_W_b': (0.0, 0.1)}
    factors = {}
    for name, (base, spread) in spreads.items():
        noise = np.random.default_rng([zlib.crc32(name.encode()), seed]).standard_normal(out[name].shape)
        drawn = base * np.exp(spread * noise) if base else spread * noise
        out[name] = jnp.asarray(drawn.astype(out[name].dtype))
    for name, factor in factors.items():
        out[name] = (out[name] * factor).astype(out[name].dtype)
    return out
```

```python
from contextlib import ExitStack

import concourse.bass as bass
from concourse import mybir

F32 = mybir.dt.float32
F32R = mybir.dt.float32r
ACT = mybir.ActivationFunctionType
ALU = mybir.AluOpType
AXX = mybir.AxisListType.X

P = 128
B = 4
L = 4096
CI = 64
N = 512
QW = 1024
NQ = L // QW
NT = N // P
NG = L // N
MT = QW // P
NM = NQ * MT
SCALE = float(P) ** -0.5
EPS = 1e-6
GROUP_CHANNELS = 4

SCORES_AT = {0: 0, 2: 1, 4: 2, 5: 3}
EXP_AT = {1: 0, 3: 1, 5: 2, 6: 3}
PT_RING = 4
PV_LAG = 2
WHOLE = (0, 1)
SPLIT = (2, 3)
NW, NS = len(WHOLE), len(SPLIT)
HL_RING = 4

U_STATS = 0
U_PROJ = 1
U_Q0 = U_PROJ + NQ + 1
U_S0 = U_Q0 + 1
U_V = U_S0 + NT
U_G0 = U_V + NQ - 1
PER_G0 = NQ * NT + 1 + 3
U_PHI = U_G0 + PER_G0 * NG - NT - 1
U_TH0 = U_PHI + NQ
U_G1 = U_TH0 + 1
PER_G1 = NQ * NT + 2
U_OUT = U_G1 + PER_G1 * NG
USES = U_OUT + NQ
CREDIT = 1
assert USES % 2 == 0 and PER_G0 % 2 == 0 and PER_G1 % 2 == 0


def score_use_0(q, t):
    return q * NT + t + (1 if q == NQ - 1 else 0)


PREV_S = U_G0 + score_use_0(NQ - 1, 0) - PER_G0
assert PREV_S == U_S0
U_QPROJ = (NQ - 1) * NT


def w_use(j, last):
    return (NQ - 1) * NT + j if last else NQ * NT + 1 + j


def score_use_1(n):
    return n + (n >= 4) + (n >= 12)


U_TH, U_G = 4, 13


def build(nc, x, out, w):
    with ExitStack() as ctx:
        def sb(name, shape, dt=F32):
            return ctx.enter_context(nc.sbuf_tensor(name, shape, dt))

        def sem(name):
            return ctx.enter_context(nc.semaphore(name))

        slot = [ctx.enter_context(nc.psum_tensor(f"score_slot{i}", [P, QW], F32)) for i in range(2)]
        pair = [ctx.enter_context(nc.psum_tensor(f"bank_pair{i}", [P, QW], F32)) for i in range(2)]
        t_bank = [pair[0][:, i * N:(i + 1) * N] for i in range(2)]
        o_bank = [pair[1][:, i * N:(i + 1) * N] for i in range(2)]

        r = sb("operands_r", [P, 4 * L + 2 * N + PT_RING * 2 * N], F32R)
        kh, kl = r[:, 0:L], r[:, L:2 * L]
        vh, vl = r[:, 2 * L:3 * L], r[:, 3 * L:4 * L]
        o = 4 * L
        qh, ql = r[:, o:o + N], r[:, o + N:o + 2 * N]
        th, tn = qh, ql
        o += 2 * N
        pth = [r[:, o + i * 2 * N:o + i * 2 * N + N] for i in range(PT_RING)]
        ptl = [r[:, o + i * 2 * N + N:o + (i + 1) * 2 * N] for i in range(PT_RING)]
        phh, phl = kh, kl
        hlh = [r[:, 2 * L + i * 2 * QW:2 * L + i * 2 * QW + QW] for i in range(HL_RING)]
        hll = [r[:, 2 * L + i * 2 * QW + QW:2 * L + (i + 1) * 2 * QW] for i in range(HL_RING)]
        ghl = [r[:, o + i * N:o + (i + 1) * N].rearrange("p (t c) -> p t c", t=NT) for i in range(2)]

        f = sb("work", [P, NQ, NT, QW])
        xc = f[:, 0, :, :].rearrange("p t n -> p (t n)")
        p0 = [f[:, 1 + i, :, :] for i in range(2)]
        osb = f[:, 3, 0:2, :].rearrange("p t n -> p (t n)")
        wb = f[:, 3, 2:4, :].rearrange("p t n -> p (t n)")
        xr = sb("x_residual", [P, L + N])
        acc = sb("acc", [P, L])
        xs = sb("x_stage", [P, N])
        zeros = sb("zeros", [P, N])
        gsb = sb("g_rows", [P, NT * CI])
        gtmp = sb("g_weighted", [P, NS * CI])
        gwh = [sb(f"g_whole{i}", [P, NW, P]) for i in range(2)]

        ident, gmat, ones = sb("ident", [P, P]), sb("gmat", [P, P]), sb("ones", [P, P])
        identr = sb("identr", [P, P], F32R)
        wq, wqs, wk, wv, wo, wvo = [sb(n + "_sb", [P, P]) for n in ("wq", "wqs", "wk", "wv", "wo", "wvo")]
        wth, wph, wout = [sb(n, [P, P]) for n in ("wth_sb", "wph_sb", "wout_sb")]
        wg = sb("wg_sb", [P, CI])
        vec = sb("vec", [P, 16])
        gamma, beta, bq, bk, bv, bo, bth, bph, bout = [vec[:, i:i + 1] for i in range(9)]
        qb, kb, vb, zero, eps = [vec[:, i:i + 1] for i in range(9, 14)]
        gbrow, gbb = sb("gbrow_sb", [1, CI]), sb("gbb", [P, CI])

        bst, mv = sb("bst", [P, NG, 6]), sb("mv", [P, 2])
        gn = sb("gn", [P, 8])
        dmean, e2, std, rstd, gmean, gain = [gn[:, i:i + 1] for i in range(6)]
        st0 = sb("st0", [P, 8 * 16])
        nm_first, z_first = st0[:, 0:NT], st0[:, NT:2 * NT]
        nmg = st0[:, 16:32].rearrange("p (q t) -> p q t", q=NQ)
        zg = st0[:, 32:48].rearrange("p (q t) -> p q t", q=NQ)
        nmin, zsum, zrec = st0[:, 8:12], st0[:, 12:16], st0[:, 48:52]
        diff, efac = st0[:, 64:80], st0[:, 80:96]
        ez, wgt = st0[:, 96:112], st0[:, 112:128]
        whr = sb("w_hi", [P, 16], F32R)
        wlr = sb("w_lo", [P, 16], F32R)
        st1 = sb("st1", [P, 8 * 16])
        nm1 = st1[:, 0:16].rearrange("p (q t) -> p q t", q=NQ)
        z1 = st1[:, 16:32].rearrange("p (q t) -> p q t", q=NQ)
        nmin1, zsum1, zrec1 = st1[:, 32:36], st1[:, 36:40], st1[:, 40:44]
        diff1, efac1, ez1, wgt1 = [st1[:, 48 + 16 * i:64 + 16 * i] for i in range(4)]

        def qt(a):
            return a.rearrange("p (q t) -> p q t", q=NQ)

        def tq(a):
            return a.rearrange("p q t -> p t q")

        s_wl = sem("weights_loaded")
        s_const, s_setup_pe, s_setup = sem("constants"), sem("setup_products"), sem("setup_done")
        s_full = [sem(f"slot_full{i}") for i in range(2)]
        s_free = [sem(f"slot_free{i}") for i in range(2)]
        s_x = [sem(f"x_loaded{i}") for i in range(NQ)]
        s_bs, s_mv, s_gm, s_dm, s_e2, s_std, s_rstd, s_gain = [
            sem(n) for n in ("chunk_stats", "channel_stats", "group_mean", "mean_offset", "second_moment",
                             "std", "rstd", "gain")]
        s_xcopy, s_xn = sem("x_copied"), sem("x_normalised")
        s_ph = sem("projection_hi")
        s_qhi = sem("q_hi")
        s_max, s_cp = sem("max0"), sem("first_quarter_stats")
        s_t = [sem(f"transposed{i}") for i in range(2)]
        s_hi = sem("pt_hi")
        s_lo = [sem(f"pt_lo{i}") for i in range(2)]
        s_pv = [sem(f"pv_done{i}") for i in range(PT_RING)]
        s_oev = [sem(f"sum_evacuated{i}") for i in range(2)]
        s_mn, s_df, s_e, s_ez, s_zs, s_zr, s_w, s_wh, s_wlo = [
            sem(n) for n in ("nmin0", "diff0", "efac0", "ez0", "zsum0", "zrec0", "wgt0", "w_hi0", "w_lo0")]
        s_wb = sem("weights_broadcast")
        s_pr, s_h1, s_h2, s_x1 = sem("weighted"), sem("half_sum"), sem("quarter_sum"), sem("x1_group")
        s_phi = sem("phi_hi")
        s_thh, s_th, s_xs, s_gs = sem("theta_hi"), sem("theta_staged"), sem("x_staged"), sem("g_rows_ready")
        s_az = sem("acc_zeroed")
        s_max1, s_hi1, s_lo1 = sem("max1"), sem("p1_hi"), sem("p1_lo")
        s_mn1, s_df1, s_e1, s_ez1, s_zs1, s_zr1, s_w1 = [
            sem(n) for n in ("nmin1", "diff1", "efac1", "ez1", "zsum1", "zrec1", "wgt1")]
        s_gw, s_gt, s_gh, s_g = sem("g_whole_ready"), sem("g_weighted"), sem("g_hi"), sem("g_ready")
        s_pvs = [sem(f"pv1_split{i}") for i in range(HL_RING)]
        s_pvf = sem("pv1_whole")
        s_acc = [sem(f"acc_added{i}") for i in range(2)]
        s_out = sem("stored")

        class Groups:

            def __init__(self, eng, b, g, groups):
                self.eng, self.made = eng, {}
                self.run, self.off = (b * groups, g) if isinstance(g, int) else (b * groups + g, 0)

            def __call__(self, k, n):
                if k not in self.made:
                    self.made[k] = self.eng.snap(self.run * k)
                return self.made[k] + (self.off * k + n)

        class Uses:

            def __init__(self, eng, b, g=0, per=0):
                fixed = isinstance(g, int)
                run = b * (USES // 2) if fixed else b * (USES // 2) + g * (per // 2)
                self.base = run if isinstance(run, int) else eng.snap(run)
                self.off = g * (per // 2) if fixed else 0

            def before(self, u):
                return self.base + (CREDIT + self.off + u // 2)

            def done(self, u):
                return self.base + (self.off + u // 2 + 1)

        def wait_full(eng, uses, u):
            eng.wait_ge(s_full[u % 2], uses.done(u))

        def wait_given_up(eng, uses, u):
            eng.wait_ge(s_free[u % 2], uses.before(u) + 1)

        def pool_copy(dst, src, n):
            return nc.gpsimd.tensor_tensor(dst, src, n, ALU.add)

        block = ctx.enter_context(nc.Block())

        @block.sync
        def _(sp):
            for s in (*s_free, *s_lo, *s_oev, *s_pv, *s_t, *s_pvs, *s_acc, s_pr, s_h1, s_h2):
                sp.sem_inc(s, CREDIT)
            sp.sem_inc(s_out, 16 * CREDIT)
            for dst, src in w:
                tile = {"wq": wq, "wk": wk, "wv": wv, "wo": wo, "wg": wg, "gbrow": gbrow, "gamma": gamma,
                        "beta": beta, "bq": bq, "bk": bk, "bv": bv, "bo": bo, "bout": bout,
                        "wth0": wth[:, 0:CI], "wth1": wth[:, CI:P], "wph0": wph[:, 0:CI], "wph1": wph[:, CI:P],
                        "wout0": wout[0:CI, :], "wout1": wout[CI:P, :],
                        "bth0": vec[0:CI, 6:7], "bth1": vec[CI:P, 6:7],
                        "bph0": vec[0:CI, 7:8], "bph1": vec[CI:P, 7:8]}[dst]
                sp.dma_start(tile[:, :] if hasattr(tile, "name") else tile, src).then_inc(s_wl, 16)

            def load(b):
                for c in range(NQ):
                    sp.dma_start(xc[:, c * QW:(c + 1) * QW], x[b, :, c * QW:(c + 1) * QW]).then_inc(s_x[c], 16)

            def store(b):
                uses = Uses(sp, b)
                for c in range(NQ):
                    wait_given_up(sp, uses, U_OUT + c)
                    sp.dma_start(out[b, :, c * QW:(c + 1) * QW], xr[:, c * QW:(c + 1) * QW]).then_inc(s_out, 16)

            load(0)
            with sp.Fori(0, B - 1) as b:
                sp.wait_ge(s_pvs[NS - 1], b * (NG * NQ * NS // HL_RING) + (NG - 1) * (NQ * NS // HL_RING) + 1 + CREDIT)
                load(b + 1)
                store(b)
            store(B - 1)
            sp.wait_ge(s_out, 16 * (NQ * B + CREDIT))

        @block.tensor
        def _(pe):
            mm = pe.matmul
            pe.wait_ge(s_wl, 16 * len(w))
            pe.wait_ge(s_const, 4)
            mm(pair[0][:, 0:P], wv[:, :], wo[:, :], start=True, stop=True)
            mm(pair[1][:, 0:1], wq[:, :], beta, start=True, stop=True)
            mm(pair[1][:, 1:2], wk[:, :], beta, start=True, stop=True)
            mm(pair[1][:, 2:2 + CI], ones[0:1, :], gbrow[:, :], start=True, stop=True).then_inc(s_setup_pe, 1)
            pe.wait_ge(s_setup, 1)
            mm(pair[0][:, N:N + 1], wvo[:, :], beta, start=True, stop=False)
            mm(pair[0][:, N:N + 1], wo[:, :], bv, start=False, stop=True).then_inc(s_setup_pe, 1)
            pe.wait_ge(s_setup, 2)

            def scores_0(uses, u, q, t):
                pe.wait_ge(s_free[u % 2], uses.before(u))
                s = slot[u % 2]
                for a, kk, first, last in ((qh, kh, True, False), (qh, kl, False, False), (ql, kh, False, True)):
                    for c in range(2):
                        ins = mm(s[:, c * N:(c + 1) * N], a[:, t * P:(t + 1) * P],
                                 kk[:, q * QW + c * N:q * QW + (c + 1) * N], start=first, stop=last)
                ins.then_inc(s_full[u % 2], 1)

            def qproj(uses, u, cols):
                pe.wait_ge(s_free[u % 2], uses.before(u))
                mm(slot[u % 2][:, 0:N], wqs[:, :], cols, start=True, stop=True).then_inc(s_full[u % 2], 1)

            def group_0(b, g, last):
                uses = Uses(pe, b, g, PER_G0)
                gi = Groups(pe, b, g, NG)

                def transpose(n):
                    if n % MT == 0:
                        u = U_G0 + score_use_0(n // MT - 1, 0) if n else PREV_S
                        wait_given_up(pe, uses, u + NT - 2)
                        wait_given_up(pe, uses, u + NT - 1)
                    pe.wait_ge(s_lo[n % 2], gi(NM // 2, CREDIT + n // 2))
                    for t in range(NT):
                        ins = pe.transpose(t_bank[n % 2][:, t * P:(t + 1) * P],
                                           p0[(n // MT) % 2][:, t, (n % MT) * P:(n % MT + 1) * P], ident[:, :])
                    ins.then_inc(s_t[n % 2], 1)

                def pv(n):
                    q, j = n // MT, n % MT
                    if j == 0:
                        pe.wait_ge(s_oev[q % 2], gi(2, CREDIT + q // 2))
                    pe.wait_ge(s_lo[n % 2], gi(NM // 2, CREDIT + n // 2 + 1))
                    ob, c = o_bank[q % 2], slice(n * P, (n + 1) * P)
                    mm(ob, vh[:, c], pth[n % PT_RING], start=(j == 0), stop=False)
                    mm(ob, vl[:, c], pth[n % PT_RING], start=False, stop=False)
                    mm(ob, vh[:, c], ptl[n % PT_RING], start=False, stop=(j == MT - 1)).then_inc(
                        s_pv[n % PT_RING], 1)

                def weights(j):
                    u = U_G0 + w_use(j, last)
                    if j == 0:
                        pe.wait_ge(s_wlo, gi(1, 1))
                    pe.wait_ge(s_free[u % 2], uses.before(u))
                    for i, q in enumerate(((0, 1), (2,), (3,))[j]):
                        for t in range(NT):
                            dst = slot[u % 2][:, i * N + t * P:i * N + (t + 1) * P]
                            k = q * NT + t
                            mm(dst, whr[:, k:k + 1].broadcast_to([P, P]), identr[:, :], start=True, stop=False)
                            ins = mm(dst, wlr[:, k:k + 1].broadcast_to([P, P]), identr[:, :], start=False, stop=True)
                    ins.then_inc(s_full[u % 2], 1)

                for n in range(NM):
                    q, j = n // MT, n % MT
                    transpose(n)
                    if j in SCORES_AT and not (last and q == NQ - 1):
                        t = SCORES_AT[j]
                        if q == NQ - 1 and t == 0:
                            wait_given_up(pe, uses, U_G0 + U_QPROJ)
                        scores_0(uses, U_G0 + score_use_0(q, t), (q + 1) % NQ, t)
                    if q == NQ - 2 and j == 6 and not last:
                        qproj(uses, U_G0 + U_QPROJ, xc[:, bass.ts(g + 1, N)])
                    if q == NQ - 1 and j >= 6:
                        weights(j - 6)
                    if n >= PV_LAG:
                        pv(n - PV_LAG)
                pv(NM - 2)
                weights(2)
                pv(NM - 1)

            def iteration_1(b, g, has_pv, has_scores):
                u0 = U_G1 + PER_G1
                uses = Uses(pe, b, g, PER_G1)
                gi = Groups(pe, b, g, NG)
                gth = Groups(pe, b, g, NG + 1)

                def scores(n):
                    q, t = n // NT, n % NT
                    u = u0 + score_use_1(n)
                    if q == 0:
                        pe.wait_ge(s_th, gth(NT, NT + t + 1))
                    pe.wait_ge(s_free[u % 2], uses.before(u))
                    for ph, first in ((phh, True), (phl, False)):
                        for c in range(2):
                            ins = mm(slot[u % 2][:, c * N:(c + 1) * N], th[:, t * P:(t + 1) * P],
                                     ph[:, q * QW + c * N:q * QW + (c + 1) * N], start=first, stop=not first)
                    ins.then_inc(s_full[u % 2], 1)

                def theta():
                    u = u0 + U_TH
                    pe.wait_ge(s_free[u % 2], uses.before(u))
                    mm(slot[u % 2][:, 0:N], wth[:, :], xr[:, bass.ds(g * N + 2 * N, N)],
                       start=True, stop=True).then_inc(s_full[u % 2], 1)

                def grows():
                    u = u0 + U_G
                    pe.wait_ge(s_xs, gi(1, 2))
                    pe.wait_ge(s_free[u % 2], uses.before(u))
                    for t in range(NT):
                        ins = mm(slot[u % 2][:, t * CI:(t + 1) * CI], xs[:, t * P:(t + 1) * P], wg[:, :],
                                 start=True, stop=True)
                    ins.then_inc(s_full[u % 2], 1)

                def pv(n):
                    q, t = n // NT, n % NT
                    a = pair[q % 2]
                    if t == 0:
                        pe.wait_ge(s_gw, gi(NQ, q + 1))
                        pe.wait_ge(s_acc[q % 2], gi(2, CREDIT + q // 2))
                    if t in WHOLE:
                        for c in range(2):
                            ins = mm(a[:, c * N:(c + 1) * N], gwh[q % 2][:, t, :],
                                     f[:, q, t, c * N:(c + 1) * N], start=(t == 0), stop=False)
                        ins.then_inc(s_pvf, 1)
                    else:
                        m = q * NS + t - NW
                        if t == NW:
                            pe.wait_ge(s_g, gi(NQ, q + 1))
                        pe.wait_ge(s_lo1, gi(NQ * NS, m + 1))
                        for part in (hlh, hll):
                            for c in range(2):
                                ins = mm(a[:, c * N:(c + 1) * N], ghl[q % 2][:, t - NW, :],
                                         part[m % HL_RING][:, c * N:(c + 1) * N],
                                         start=False, stop=(t == NT - 1 and part is hll))
                        ins.then_inc(s_pvs[m % HL_RING], 1)

                for q in range(NQ):
                    first = q * NT
                    if has_pv and has_scores:
                        order = {0: "SSPPPSPS", NQ - 1: "PSPSSPSP"}.get(q, "PSPSPSPS")
                    else:
                        order = "SSSS" if has_scores else "PPPP"
                    ns = np_ = 0
                    for what in order:
                        if what == "P":
                            pv(first + np_)
                            np_ += 1
                            continue
                        if (q, ns) == (1, 0):
                            theta()
                        if (q, ns) == (NQ - 1, 0):
                            grows()
                        scores(first + ns)
                        ns += 1
                    if not has_scores and q > 0:
                        project_out(b, q - 1)

            def project_out(b, c):
                uses = Uses(pe, b)
                u = U_OUT + c
                pe.wait_ge(s_acc[c % 2], b * (NG * 2) + (NG - 1) * 2 + c // 2 + 1 + CREDIT)
                pe.wait_ge(s_free[u % 2], uses.before(u))
                for i in range(2):
                    ins = mm(slot[u % 2][:, i * N:(i + 1) * N], wout[:, :],
                             acc[:, c * QW + i * N:c * QW + (i + 1) * N], start=True, stop=True)
                ins.then_inc(s_full[u % 2], 1)

            with pe.Fori(0, B) as b:
                uses = Uses(pe, b)
                u = U_STATS
                pe.wait_ge(s_mv, b + 1)
                pe.wait_ge(s_free[u % 2], uses.before(u))
                mm(slot[u % 2][:, 0:1], gmat[:, :], mv[:, 0:1], start=True, stop=True).then_inc(s_gm, 1)
                pe.wait_ge(s_e2, b + 1)
                mm(slot[u % 2][:, N:N + 1], gmat[:, :], e2, start=True, stop=True).then_inc(s_full[u % 2], 1)

                def project(u, c, is_k):
                    pe.wait_ge(s_xn, b * NQ + c + 1)
                    pe.wait_ge(s_free[u % 2], uses.before(u))
                    if is_k:
                        for i in range(2):
                            ins = mm(slot[u % 2][:, i * N:(i + 1) * N], wk[:, :],
                                     xc[:, c * QW + i * N:c * QW + (i + 1) * N], start=True, stop=True)
                    else:
                        for i in range(MT):
                            ins = mm(slot[u % 2][:, i * P:(i + 1) * P], xc[:, c * QW + i * P:c * QW + (i + 1) * P],
                                     wvo[:, :], start=True, stop=True)
                    ins.then_inc(s_full[u % 2], 1)

                for c in range(NQ):
                    project(U_PROJ + c, c, True)
                project(U_PROJ + NQ, 0, False)
                qproj(uses, U_Q0, xc[:, 0:N])
                wait_given_up(pe, uses, U_Q0)
                for t in range(NT):
                    scores_0(uses, U_S0 + t, 0, t)
                for c in range(1, NQ):
                    project(U_V + c - 1, c, False)
                with pe.Fori(0, NG - 1) as g:
                    group_0(b, g, False)
                group_0(b, NG - 1, True)

                pe.wait_ge(s_x1, b * NG + NG)
                for c in range(NQ):
                    u = U_PHI + c
                    pe.wait_ge(s_free[u % 2], uses.before(u))
                    for i in range(2):
                        ins = mm(slot[u % 2][:, i * N:(i + 1) * N], wph[:, :],
                                 xr[:, c * QW + i * N:c * QW + (i + 1) * N], start=True, stop=True)
                    ins.then_inc(s_full[u % 2], 1)
                u = U_TH0
                pe.wait_ge(s_free[u % 2], uses.before(u))
                mm(slot[u % 2][:, 0:N], wth[:, :], xr[:, 0:N], start=True, stop=True).then_inc(s_full[u % 2], 1)
                iteration_1(b, -1, False, True)
                with pe.Fori(0, NG - 1) as g:
                    iteration_1(b, g, True, True)
                iteration_1(b, NG - 1, True, False)
                project_out(b, NQ - 1)

        @block.scalar
        def _(act):
            def exp0(uses, u, t, nm, z, dst):
                act.activation(dst, slot[u % 2][:, :], ACT.Exp, bias=nm, accum_out=z).then_inc(s_free[u % 2], 1)

            def group_0(b, g, last):
                uses = Uses(act, b, g, PER_G0)
                gi = Groups(act, b, g, NG)

                def hi(n):
                    act.wait_ge(s_t[n % 2], gi(NM // 2, CREDIT + n // 2 + 1))
                    act.wait_ge(s_pv[n % PT_RING], gi(NM // PT_RING, CREDIT + n // PT_RING))
                    act.activation(pth[n % PT_RING], t_bank[n % 2], ACT.Copy).then_inc(s_hi, 1)

                def sum_out(q):
                    n = q * MT + MT - 1
                    act.wait_ge(s_h1, gi(1, CREDIT + 0))
                    act.wait_ge(s_pv[n % PT_RING], gi(NM // PT_RING, CREDIT + n // PT_RING + 1))
                    act.activation(osb[:, q * N:(q + 1) * N], o_bank[q % 2], ACT.Copy).then_inc(s_oev[q % 2], 1)

                def weights_out(j):
                    u = U_G0 + w_use(j, last)
                    wait_full(act, uses, u)
                    act.wait_ge(s_h2, gi(1, CREDIT + 0))
                    n0, n1 = ((0, 2), (2, 3), (3, 4))[j]
                    act.activation(wb[:, n0 * N:n1 * N], slot[u % 2][:, 0:(n1 - n0) * N], ACT.Copy).then_inc(
                        s_free[u % 2], 1)

                for n in range(NM):
                    q, j = n // MT, n % MT
                    hi(n)
                    if q == NQ - 2 and j == 6 and not last:
                        wait_full(act, uses, U_G0 + U_QPROJ)
                        act.activation(qh, slot[(U_G0 + U_QPROJ) % 2][:, 0:N], ACT.Identity, bias=qb).then_inc(
                            s_qhi, 1)
                    if j in EXP_AT and not (last and q == NQ - 1):
                        t = EXP_AT[j]
                        u = U_G0 + score_use_0(q, t)
                        act.wait_ge(s_max, gi(NQ * NT, NT * (q + 1) + t + 1))
                        if t == 0:
                            act.wait_ge(s_t[1], gi(NM // 2, CREDIT + q * (MT // 2)))
                        if q == NQ - 1:
                            exp0(uses, u, t, nm_first[:, t:t + 1], z_first[:, t:t + 1], p0[0][:, t, :])
                        else:
                            exp0(uses, u, t, nmg[:, q + 1, t:t + 1], zg[:, q + 1, t:t + 1], p0[(q + 1) % 2][:, t, :])
                    if q == NQ - 1 and j == 2:
                        act.wait_ge(s_df, gi(1, 1))
                        act.activation(efac, diff, ACT.Exp).then_inc(s_e, 1)
                    if j == PV_LAG + 1 and q > 0:
                        sum_out(q - 1)
                weights_out(0)
                weights_out(1)
                weights_out(2)
                sum_out(NQ - 1)

            def iteration_1(b, g, has_pv, has_scores):
                u0 = U_G1 + PER_G1
                uses = Uses(act, b, g, PER_G1)
                gi, gth = Groups(act, b, g, NG), Groups(act, b, g, NG + 1)

                def hi(n):
                    q, t = n // NT, n % NT
                    if t in SPLIT:
                        m = q * NS + t - NW
                        wait_given_up(act, uses, u0 - PER_G1 + score_use_1(n))
                        act.wait_ge(s_pvs[m % HL_RING], gi(NQ * NS // HL_RING, CREDIT + m // HL_RING))
                        act.activation(hlh[m % HL_RING], f[:, q, t, :], ACT.Copy).then_inc(s_hi1, 1)

                def theta_hi():
                    u = u0 + U_TH
                    wait_full(act, uses, u)
                    act.wait_ge(s_th, gth(NT, 2 * NT))
                    act.activation(tn, slot[u % 2][:, 0:N], ACT.Identity, bias=bth).then_inc(s_thh, 1)

                def exp1(n):
                    q, t = n // NT, n % NT
                    u = u0 + score_use_1(n)
                    act.wait_ge(s_max1, gi(NQ * NT, NQ * NT + n + 1))
                    if has_pv and t in WHOLE:
                        act.wait_ge(s_pvf, gi(NQ * NW, q * NW + t + 1))
                    elif has_pv:
                        act.wait_ge(s_lo1, gi(NQ * NS, q * NS + t - NW + 1))
                    act.activation(f[:, q, t, :], slot[u % 2][:, :], ACT.Exp, bias=nm1[:, q, t:t + 1],
                                   accum_out=z1[:, q, t:t + 1]).then_inc(s_free[u % 2], 1)

                if has_pv:
                    hi(NW)
                for q in range(NQ):
                    n = q * NT
                    if has_pv:
                        hi(n + NW + 1)
                    if has_scores:
                        if q == 1:
                            theta_hi()
                        exp1(n)
                        exp1(n + 1)
                    if has_pv and q < NQ - 1:
                        hi(n + NT + NW)
                    if has_scores:
                        exp1(n + 2)
                        exp1(n + 3)
                if has_scores:
                    act.wait_ge(s_df1, gi(1, 2))
                    act.activation(efac1, diff1, ACT.Exp).then_inc(s_e1, 1)

            act.wait_ge(s_setup, 2)
            with act.Fori(0, B) as b:
                uses = Uses(act, b)
                act.wait_ge(s_out, b * (16 * NQ) + 16 * CREDIT)
                for c in range(NQ):
                    act.wait_ge(s_x[c], b * 16 + 16)
                    act.activation(xr[:, c * QW:(c + 1) * QW], xc[:, c * QW:(c + 1) * QW], ACT.Identity,
                                   bias=vb).then_inc(s_xcopy, 1)
                wait_full(act, uses, U_STATS)
                act.activation(std, slot[U_STATS % 2][:, N:N + 1], ACT.Sqrt, bias=eps).then_inc(s_std, 1)

                def high(u, dst, bias):
                    wait_full(act, uses, u)
                    act.activation(dst, slot[u % 2][:, :], ACT.Identity, bias=bias).then_inc(s_ph, 1)

                for c in range(NQ):
                    high(U_PROJ + c, kh[:, c * QW:(c + 1) * QW], kb)
                high(U_PROJ + NQ, vh[:, 0:QW], zero)
                wait_full(act, uses, U_Q0)
                act.activation(qh, slot[U_Q0 % 2][:, 0:N], ACT.Identity, bias=qb).then_inc(s_qhi, 1)
                for t in range(NT):
                    act.wait_ge(s_max, b * (NG * NQ * NT) + t + 1)
                    exp0(uses, U_S0 + t, t, nm_first[:, t:t + 1], z_first[:, t:t + 1], p0[0][:, t, :])
                for c in range(1, NQ):
                    high(U_V + c - 1, vh[:, c * QW:(c + 1) * QW], zero)
                with act.Fori(0, NG - 1) as g:
                    group_0(b, g, False)
                group_0(b, NG - 1, True)

                for c in range(NQ):
                    u = U_PHI + c
                    wait_full(act, uses, u)
                    act.activation(phh[:, c * QW:(c + 1) * QW], slot[u % 2][:, :], ACT.Identity,
                                   bias=bph).then_inc(s_phi, 1)
                wait_full(act, uses, U_TH0)
                act.activation(tn, slot[U_TH0 % 2][:, 0:N], ACT.Identity, bias=bth).then_inc(s_thh, 1)
                iteration_1(b, -1, False, True)
                with act.Fori(0, NG - 1) as g:
                    iteration_1(b, g, True, True)
                iteration_1(b, NG - 1, True, False)

        @block.vector
        def _(dve):
            def minus(dst, src, bias, high):
                return dve.scalar_tensor_tensor(out=dst, in0=src, scalar=bias, in1=high.bitcast(F32),
                                                op0=ALU.add, op1=ALU.subtract)

            dve.memset(zero, 0.0)
            dve.memset(eps, EPS)
            dve.memset(xr[:, L:L + N], 0.0).then_inc(s_const, 1)
            dve.wait_ge(s_const, 4)
            dve.tensor_copy(identr[:, :], ident[:, :])
            dve.wait_ge(s_wl, 16 * len(w))
            dve.tensor_scalar(wqs[:, :], wq[:, :], SCALE, None, ALU.mult)
            dve.wait_ge(s_setup_pe, 1)
            dve.tensor_copy(wvo[:, :], pair[0][:, 0:P]).then_inc(s_setup, 1)
            dve.tensor_scalar(qb, pair[1][:, 0:1], bq, SCALE, ALU.add, ALU.mult)
            dve.tensor_tensor(kb, pair[1][:, 1:2], bk, ALU.add)
            dve.tensor_copy(gbb[:, :], pair[1][:, 2:2 + CI])
            dve.wait_ge(s_setup_pe, 2)
            dve.tensor_tensor(vb, pair[0][:, N:N + 1], bo, ALU.add).then_inc(s_setup, 1)

            def softmax_weights(i, nm, z, nmn, df, e, ezt, zs, zr, wt, s):
                s_mn_, s_df_, s_e_, s_ez_, s_zs_, s_zr_, s_w_ = s
                if df is not None:
                    dve.tensor_reduce(nmn, tq(nm), AXX, ALU.min).then_inc(s_mn_, 1)
                    dve.wait_ge(s_mn_, i(1, 1))
                    dve.tensor_tensor(qt(df), nmn.unsqueeze(1).broadcast_to([P, NQ, NT]), nm,
                                      ALU.subtract).then_inc(s_df_, 1)
                if e is not None:
                    dve.wait_ge(s_e_, i(1, 1))
                    dve.tensor_tensor(qt(ezt), qt(e), z, ALU.mult).then_inc(s_ez_, 1)
                    dve.wait_ge(s_ez_, i(1, 1))
                    dve.tensor_reduce(zs, tq(qt(ezt)), AXX, ALU.add).then_inc(s_zs_, 1)
                    dve.wait_ge(s_zs_, i(1, 1))
                    dve.reciprocal(zr, zs).then_inc(s_zr_, 1)
                    dve.wait_ge(s_zr_, i(1, 1))
                    dve.tensor_tensor(qt(wt), qt(e), zr.unsqueeze(1).broadcast_to([P, NQ, NT]),
                                      ALU.mult).then_inc(s_w_, 1)

            def group_0(b, g, last):
                uses = Uses(dve, b, g, PER_G0)
                gi = Groups(dve, b, g, NG)
                chain = (s_mn, s_df, s_e, s_ez, s_zs, s_zr, s_w)

                def lo(n):
                    dve.wait_ge(s_hi, gi(NM, n + 1))
                    dve.tensor_tensor(ptl[n % PT_RING], t_bank[n % 2], pth[n % PT_RING].bitcast(F32),
                                      ALU.subtract).then_inc(s_lo[n % 2], 1)

                for n in range(NM):
                    q, j = n // MT, n % MT
                    lo(n)
                    if q == NQ - 2 and j == 6 and not last:
                        dve.wait_ge(s_qhi, gi(1, 2))
                        u = U_G0 + U_QPROJ
                        minus(ql, slot[u % 2][:, 0:N], qb, qh).then_inc(s_free[u % 2], 1)
                    if j in SCORES_AT and not (last and q == NQ - 1):
                        t = SCORES_AT[j]
                        u = U_G0 + score_use_0(q, t)
                        wait_full(dve, uses, u)
                        dst = nm_first[:, t:t + 1] if q == NQ - 1 else nmg[:, q + 1, t:t + 1]
                        dve.tensor_reduce(dst, slot[u % 2][:, :], AXX, ALU.max, negate=True).then_inc(s_max, 1)
                    if q == 0 and j == 1:
                        wait_given_up(dve, uses, PREV_S + NT - 2)
                        wait_given_up(dve, uses, PREV_S + NT - 1)
                        dve.tensor_copy(nmg[:, 0, :], nm_first).then_inc(s_cp, 1)
                        dve.tensor_copy(zg[:, 0, :], z_first).then_inc(s_cp, 1)
                    if q == NQ - 1 and j == 1:
                        u = U_G0 + score_use_0(NQ - 2, NT - 1)
                        wait_given_up(dve, uses, u - 1)
                        wait_given_up(dve, uses, u)
                        dve.wait_ge(s_cp, gi(2, 2))
                        softmax_weights(gi, nmg, zg, nmin, diff, None, None, None, None, None, chain)
                    if q == NQ - 1 and j == 3:
                        softmax_weights(gi, None, zg, None, None, efac, ez, zsum, zrec, wgt, chain)
                        dve.wait_ge(s_w, gi(1, 1))
                        dve.wait_ge(s_pr, gi(1, CREDIT + 0))
                        dve.tensor_copy(whr[:, :], wgt).then_inc(s_wh, 1)
                        dve.wait_ge(s_wh, gi(1, 1))
                        dve.tensor_tensor(wlr[:, :], wgt, whr[:, :].bitcast(F32), ALU.subtract).then_inc(s_wlo, 1)

            def iteration_1(b, g, has_pv, has_scores):
                u0 = U_G1 + PER_G1
                uses = Uses(dve, b, g, PER_G1)
                gi, gth = Groups(dve, b, g, NG), Groups(dve, b, g, NG + 1)

                nxt = Groups(dve, b, g + 1, NG)

                def add_sum(q):
                    m = q * NS + NS - 1
                    dve.wait_ge(s_pvs[m % HL_RING], gi(NQ * NS // HL_RING, CREDIT + m // HL_RING + 1))
                    dve.wait_ge(s_acc[q % 2], gi(2, CREDIT + q // 2))
                    dve.tensor_tensor(acc[:, q * QW:(q + 1) * QW], pair[q % 2][:, :], acc[:, q * QW:(q + 1) * QW],
                                      ALU.add).then_inc(s_acc[q % 2], 1)

                def lo(n):
                    q, t = n // NT, n % NT
                    m = q * NS + t - NW
                    dve.wait_ge(s_hi1, gi(NQ * NS, m + 1))
                    dve.tensor_tensor(hll[m % HL_RING], f[:, q, t, :], hlh[m % HL_RING].bitcast(F32),
                                      ALU.subtract).then_inc(s_lo1, 1)

                def maximum(n):
                    u = u0 + score_use_1(n)
                    wait_full(dve, uses, u)
                    dve.tensor_reduce(nm1[:, n // NT, n % NT:n % NT + 1], slot[u % 2][:, :], AXX, ALU.max,
                                      negate=True).then_inc(s_max1, 1)

                def theta_lo():
                    u = u0 + U_TH
                    dve.wait_ge(s_thh, gth(1, 3))
                    minus(tn[CI:P, :], slot[u % 2][CI:P, 0:N], bth[CI:P, :], tn[CI:P, :]).then_inc(s_free[u % 2], 1)

                def g_rows():
                    u = u0 + U_G
                    wait_full(dve, uses, u)
                    if has_pv:
                        dve.wait_ge(s_g, gi(NQ, NQ))
                    dve.tensor_tensor(gsb[:, :].rearrange("p (t c) -> p t c", t=NT),
                                      slot[u % 2][:, 0:NT * CI].rearrange("p (t c) -> p t c", t=NT),
                                      gbb[:, :].unsqueeze(1).broadcast_to([P, NT, CI]),
                                      ALU.add).then_inc(s_free[u % 2], 1)

                for q in range(NQ):
                    n = q * NT
                    if has_pv:
                        lo(n + NW)
                    if has_scores:
                        if q == 1:
                            theta_lo()
                        if q == NQ - 1:
                            g_rows()
                        maximum(n)
                    if has_pv:
                        lo(n + NW + 1)
                    if has_scores:
                        maximum(n + 1)
                    if has_pv and q > 0:
                        add_sum(q - 1)
                        if not has_scores and q > 1:
                            final_sum(b, q - 2)
                    if has_scores:
                        maximum(n + 2)
                        maximum(n + 3)
                if has_scores:
                    for v in (2, 3):
                        wait_given_up(dve, uses, u0 + score_use_1((NQ - 1) * NT + v))
                    softmax_weights(nxt, nm1, z1, nmin1, diff1, efac1, ez1, zsum1, zrec1, wgt1,
                                    (s_mn1, s_df1, s_e1, s_ez1, s_zs1, s_zr1, s_w1))
                if has_pv:
                    add_sum(NQ - 1)

            def final_sum(b, c):
                uses = Uses(dve, b)
                u = U_OUT + c
                wait_full(dve, uses, u)
                cols = xr[:, c * QW:(c + 1) * QW]
                dve.scalar_tensor_tensor(out=cols, in0=slot[u % 2][:, :], scalar=bout, in1=cols,
                                         op0=ALU.add, op1=ALU.add).then_inc(s_free[u % 2], 1)

            dve.wait_ge(s_setup, 2)
            with dve.Fori(0, B) as b:
                uses = Uses(dve, b)
                for c in range(NG):
                    if c % 2 == 0:
                        dve.wait_ge(s_x[c // 2], b * 16 + 16)
                    dve.bn_stats(bst[:, c, :], xc[:, c * N:(c + 1) * N]).then_inc(s_bs, 1)
                dve.wait_ge(s_bs, b * NG + NG)
                dve.memset(gn[:, 6:7], 0.0)
                dve.bn_aggr(mv[:, :], bst[:, :, :]).then_inc(s_mv, 1)
                u = U_STATS
                dve.wait_ge(s_gm, b + 1)
                dve.wait_ge(s_mv, b + 1)
                dve.tensor_tensor(dmean, mv[:, 0:1], slot[u % 2][:, 0:1], ALU.subtract).then_inc(s_dm, 1)
                dve.wait_ge(s_dm, b + 1)
                dve.scalar_tensor_tensor(out=e2, in0=dmean, scalar=dmean, in1=mv[:, 1:2], op0=ALU.mult,
                                         op1=ALU.add).then_inc(s_e2, 1)
                dve.wait_ge(s_std, b + 1)
                dve.reciprocal(rstd, std).then_inc(s_rstd, 1)
                dve.tensor_copy(gmean, slot[u % 2][:, 0:1]).then_inc(s_free[u % 2], 1)
                dve.wait_ge(s_rstd, b + 1)
                dve.tensor_tensor(gain, rstd, gamma, ALU.mult).then_inc(s_gain, 1)
                dve.wait_ge(s_gain, b + 1)
                wait_given_up(dve, uses, u)
                for c in range(NQ):
                    dve.wait_ge(s_xcopy, b * NQ + c + 1)
                    cols = xc[:, c * QW:(c + 1) * QW]
                    dve.tensor_scalar(cols, cols, gmean, gain, ALU.subtract, ALU.mult).then_inc(s_xn, 1)

                def low(u, j, src, dst, bias):
                    dve.wait_ge(s_ph, b * (2 * NQ) + j + 1)
                    minus(dst, slot[u % 2][:, :], bias, src).then_inc(s_free[u % 2], 1)

                for c in range(NQ):
                    low(U_PROJ + c, c, kh[:, c * QW:(c + 1) * QW], kl[:, c * QW:(c + 1) * QW], kb)
                low(U_PROJ + NQ, NQ, vh[:, 0:QW], vl[:, 0:QW], zero)
                dve.wait_ge(s_qhi, b * NG + 1)
                minus(ql, slot[U_Q0 % 2][:, 0:N], qb, qh).then_inc(s_free[U_Q0 % 2], 1)
                for t in range(NT):
                    wait_full(dve, uses, U_S0 + t)
                    dve.tensor_reduce(nm_first[:, t:t + 1], slot[(U_S0 + t) % 2][:, :], AXX, ALU.max,
                                      negate=True).then_inc(s_max, 1)
                for c in range(1, NQ):
                    low(U_V + c - 1, NQ + c, vh[:, c * QW:(c + 1) * QW], vl[:, c * QW:(c + 1) * QW], zero)
                with dve.Fori(0, NG - 1) as g:
                    group_0(b, g, False)
                group_0(b, NG - 1, True)

                for c in range(NQ):
                    u = U_PHI + c
                    cols = slice(c * QW, (c + 1) * QW)
                    dve.wait_ge(s_phi, b * NQ + c + 1)
                    minus(phl[:, cols], slot[u % 2][:, :], bph, phh[:, cols]).then_inc(s_free[u % 2], 1)
                dve.wait_ge(s_thh, b * (NG + 1) + 1)
                minus(tn[CI:P, :], slot[U_TH0 % 2][CI:P, 0:N], bth[CI:P, :], tn[CI:P, :]).then_inc(
                    s_free[U_TH0 % 2], 1)
                dve.wait_ge(s_az, b + 1)
                iteration_1(b, -1, False, True)
                with dve.Fori(0, NG - 1) as g:
                    iteration_1(b, g, True, True)
                iteration_1(b, NG - 1, True, False)
                for c in (NQ - 2, NQ - 1):
                    final_sum(b, c)

        @block.gpsimd
        def _(pool):
            pool.memset(ident[:, :], 0.0).then_inc(s_const, 1)
            pool.memset(gmat[:, :], 1.0 / GROUP_CHANNELS)
            pool.memset(ones[:, :], 1.0)
            pool.memset(zeros[:, :], 0.0)
            for i in range(2):
                pool.memset(gwh[i][:, :, :], 0.0)
            blocks = gmat[:, :].rearrange("p (a c) -> p a c", c=GROUP_CHANNELS)
            pool.drain().then_inc(s_const, 1)
            pool.wait_ge(s_const, 3)
            pool.affine_select(out=ident[:, :], in_=ident[:, :], compare_op=ALU.not_equal, fill=1.0, base=0,
                               pattern=[[-1, P]], channel_multiplier=1)
            pool.affine_select(out=blocks, in_=blocks, compare_op=ALU.is_ge, fill=0.0, base=0,
                               pattern=[[-GROUP_CHANNELS, P // GROUP_CHANNELS], [0, GROUP_CHANNELS]],
                               channel_multiplier=1).then_inc(s_gt, 1)
            pool.wait_ge(s_gt, 1)
            pool.affine_select(out=blocks, in_=blocks, compare_op=ALU.is_ge, fill=0.0, base=GROUP_CHANNELS - 1,
                               pattern=[[GROUP_CHANNELS, P // GROUP_CHANNELS], [0, GROUP_CHANNELS]],
                               channel_multiplier=-1).then_inc(s_const, 1)

            def group_0(b, g, last):
                uses = Uses(pool, b, g, PER_G0)
                gi = Groups(pool, b, g, NG)
                for j in range(3):
                    wait_given_up(pool, uses, U_G0 + w_use(j, last))
                for i in range(2):
                    pool.wait_ge(s_oev[i], gi(2, CREDIT + 2))
                pool.tensor_tensor(osb, osb, wb, ALU.mult).then_inc(s_pr, 1)
                pool.wait_ge(s_pr, gi(1, CREDIT + 1))
                pool.tensor_tensor(wb[:, 0:QW], osb[:, 0:QW], osb[:, QW:2 * QW], ALU.add).then_inc(s_h1, 1)
                pool.wait_ge(s_h1, gi(1, CREDIT + 1))
                pool.tensor_tensor(xs[:, :], wb[:, 0:N], wb[:, N:2 * N], ALU.add).then_inc(s_h2, 1)
                pool.wait_ge(s_h2, gi(1, CREDIT + 1))
                cols = xr[:, bass.ts(g, N)] if not last else xr[:, g * N:(g + 1) * N]
                pool.tensor_tensor(cols, cols, xs[:, :], ALU.add).then_inc(s_x1, 1)

            def iteration_1(b, g, has_pv, has_scores):
                u0 = U_G1 + PER_G1
                uses = Uses(pool, b, g, PER_G1)
                gi = Groups(pool, b, g, NG)
                rows = gsb[:, :].rearrange("p (t c) -> p t c", t=NT)
                part = gtmp[:, :].rearrange("p (t c) -> p t c", t=NS)
                for q in range(NQ):
                    if has_pv:
                        if q == 0:
                            pool.wait_ge(s_w1, gi(1, 1))
                        pool.wait_ge(s_acc[q % 2], gi(2, CREDIT + q // 2))
                        pool.tensor_tensor(gwh[q % 2][:, :, 0:CI], rows[:, 0:NW, :],
                                           wgt1[:, q * NT:q * NT + NW].unsqueeze(2).broadcast_to([P, NW, CI]),
                                           ALU.mult).then_inc(s_gw, 1)
                        pool.tensor_tensor(part, rows[:, NW:NT, :],
                                           wgt1[:, q * NT + NW:(q + 1) * NT].unsqueeze(2).broadcast_to([P, NS, CI]),
                                           ALU.mult).then_inc(s_gt, 1)
                        pool.wait_ge(s_gt, gi(NQ, q + 2))
                        pool_copy(ghl[q % 2][:, 0:NS, 0:CI], part,
                                  zeros[:, 0:NS * CI].rearrange("p (t c) -> p t c", t=NS)).then_inc(s_gh, 1)
                        pool.wait_ge(s_gh, gi(NQ, q + 1))
                        pool.tensor_tensor(ghl[q % 2][:, 0:NS, CI:P], part, ghl[q % 2][:, 0:NS, 0:CI].bitcast(F32),
                                           ALU.subtract).then_inc(s_g, 1)
                        pool.wait_ge(s_g, gi(NQ, q + 1))
                    if has_scores and q == 1:
                        if has_pv:
                            wait_given_up(pool, uses, u0 + U_G - PER_G1)
                        else:
                            pool.wait_ge(s_x1, b * NG + NG)
                        pool_copy(xs[:, :], xr[:, bass.ds(g * N + N, N)], zeros[:, :]).then_inc(s_xs, 1)
                    if has_scores and q == NQ - 1:
                        wait_given_up(pool, uses, u0 + U_TH)
                        for t in range(NT):
                            u = u0 + score_use_1(q * NT + t)
                            pool.wait_ge(s_full[u % 2], uses.done(u))
                            pool_copy(th[:, t * P:(t + 1) * P], tn[:, t * P:(t + 1) * P].bitcast(F32),
                                      zeros[:, 0:P]).then_inc(s_th, 1)

            pool.wait_ge(s_setup, 2)
            with pool.Fori(0, B) as b:
                uses = Uses(pool, b)
                with pool.Fori(0, NG - 1) as g:
                    group_0(b, g, False)
                group_0(b, NG - 1, True)
                pool.wait_ge(s_full[U_PHI % 2], uses.done(U_PHI))
                zeros8 = zeros[:, :].unsqueeze(1).broadcast_to([P, NG, N])
                pool_copy(acc[:, :].rearrange("p (a n) -> p a n", a=NG), zeros8, zeros8).then_inc(s_az, 1)
                wait_given_up(pool, uses, U_TH0)
                for t in range(NT):
                    pool_copy(th[:, t * P:(t + 1) * P], tn[:, t * P:(t + 1) * P].bitcast(F32),
                              zeros[:, 0:P]).then_inc(s_th, 1)
                iteration_1(b, -1, False, True)
                with pool.Fori(0, NG - 1) as g:
                    iteration_1(b, g, True, True)
                iteration_1(b, NG - 1, True, False)


def kernel(**inputs):
    import numpy as np
    import concourse.bacc as bacc
    from concourse.bass_utils import run_bass_kernel_spmd as run

    nc = bacc.Bacc("TRN2", target_bir_lowering=False, num_devices=1)
    arrays = {}

    def given(name, a):
        a = np.ascontiguousarray(a)
        arrays[name] = a
        return nc.dram_tensor(name, a.shape, F32, kind="ExternalInput").ap()

    def col(a):
        return np.asarray(a).reshape(-1, 1)

    x = given("in_x", np.asarray(inputs["x"]).reshape(B, P, L))
    i0 = {k[len("L0_conv_"):]: np.asarray(v) for k, v in inputs.items() if k.startswith("L0_conv_")}
    i1 = {k[len("L1_conv_"):]: np.asarray(v) for k, v in inputs.items() if k.startswith("L1_conv_")}
    wth, bth = given("theta_w_t", i1["theta_w"].T), given("theta_b", col(i1["theta_b"]))
    wph, bph = given("phi_w_t", i1["phi_w"].T), given("phi_b", col(i1["phi_b"]))
    wout = given("W_w_t", i1["W_w"].T)
    w = [
        ("wq", given("wq_t", i0["wq"].T)), ("wk", given("wk_t", i0["wk"].T)), ("wv", given("wv", i0["wv"])),
        ("wo", given("wo_t", i0["wo"].T)), ("wg", given("g_w_t", i1["g_w"].T)),
        ("gbrow", given("g_b", i1["g_b"].reshape(1, -1))),
        ("gamma", given("gamma", col(i0["gamma"]))), ("beta", given("beta", col(i0["beta"]))),
        ("bq", given("bq", col(i0["bq"]))), ("bk", given("bk", col(i0["bk"]))),
        ("bv", given("bv", col(i0["bv"]))), ("bo", given("bo", col(i0["bo"]))),
        ("bout", given("W_b", col(i1["W_b"]))),
        ("wth0", wth), ("wth1", wth), ("wph0", wph), ("wph1", wph), ("wout0", wout), ("wout1", wout),
        ("bth0", bth), ("bth1", bth), ("bph0", bph), ("bph1", bph),
    ]
    out = nc.dram_tensor("out_0", (B, P, 64, 64), F32, kind="ExternalOutput").ap()
    build(nc, x, out.rearrange("b c h w -> b c (h w)"), w)
    r = run(nc, [arrays], core_ids=[0])
    return r.results[0]["out_0"]
```

```python
from contextlib import ExitStack

import concourse.bass as bass
from concourse import mybir

F32 = mybir.dt.float32
F32R = mybir.dt.float32r
ACT = mybir.ActivationFunctionType
ALU = mybir.AluOpType
AXX = mybir.AxisListType.X

P = 128
B = 4
L = 4096
CI = 64
N = 512
QW = 1024
NQ = L // QW
NT = N // P
NG = L // N
MT = QW // P
NM = NQ * MT
SCALE = float(P) ** -0.5
EPS = 1e-6
GROUP_CHANNELS = 4

SCORES_AT = {0: 0, 2: 1, 4: 2, 5: 3}
EXP_AT = {1: 0, 3: 1, 5: 2, 6: 3}
FIRST_1 = {(2, 6): 'phi', (2, 7): 'theta', (3, 1): 0, (3, 2): 1, (3, 3): 2, (3, 4): 3}
FIRST_EXP_1 = {(3, 2): 0, (3, 3): 1, (3, 4): 2, (3, 5): 3}
PT_RING = 4
PV_LAG = 2
WHOLE = (0, 1)
SPLIT = (2, 3)
HALVES = (slice(0, 2), slice(2, 4))
NW, NS = len(WHOLE), len(SPLIT)
HL_RING = 4
PE_ORDER = ("SPSPPSSP", "TPSPSPPSS", "PSPSPSPS", "PGSPSSPSP")
ACT_ORDER = ("H2 H3 E0 E1 H6 E2 E3".split(), "H3 T0 E0 E1 H6 E2 E3".split(), "H3 E0 E1 H6 E2 E3".split(),
             "H3 E0 E1 D0 E2 E3 D1".split())
DVE_ORDER = ("M0 L2 M1 L3 M2 M3".split(), "L2 T0 M0 L3 M1 A0 M2 M3".split(), "L2 M0 L3 M1 A1 M2 M3".split(),
             "L2 G0 M0 A2 M1 D0 M2 L3 R0 M3 W0 D1 A3 R1 W1".split())

U_PROJ = 0
U_Q0 = U_PROJ + NQ + 1
U_S0 = U_Q0 + 1
U_V = U_S0 + NT
U_G0 = U_V + NQ - 1
PER_G0 = NQ * NT + 1 + 3
U_PHI0 = U_G0 + PER_G0 * (NG - 1) + (NQ - 1) * NT
U_TH0 = U_PHI0 + 1
U_FIRST = U_TH0 + 1
U_PHI1 = U_FIRST + NT + 3
U_BEGIN = U_PHI1 + 2
BEGIN = ("theta", 4, 6, "phi", 8, 10, "g", 12, 14)
PER_G1 = NQ * NT + 2
U_G1 = U_BEGIN + len(BEGIN) - PER_G1
PAIR_USES = (NQ - 1) * NT // 4
U_OUT = U_G1 + PER_G1 * NG
U_STATS = U_OUT + 2
USES = U_OUT + NQ + 1
CREDIT = 1
assert USES % 2 == 0 and PER_G0 % 2 == 0 and PER_G1 % 2 == 0


def score_use_0(q, t):
    return q * NT + t + (1 if q == NQ - 1 else 0)


PREV_S = U_G0 + score_use_0(NQ - 1, 0) - PER_G0
assert PREV_S == U_S0
U_QPROJ = (NQ - 1) * NT


def w_use(j, last):
    return NQ * NT + 1 + j + (1 if last else 0)


def phi_use(c):
    return {0: U_PHI0, NQ - 1: U_BEGIN + BEGIN.index("phi")}.get(c, U_PHI1 + c - 1)


def out_use(c):
    return U_OUT + c + (U_OUT + c >= U_STATS)


U_TH, U_G = NT, (NQ - 1) * NT + 1


def use_1(what, first):
    return PER_G1 + (U_BEGIN + BEGIN.index(what) if first else U_G1 + {"theta": U_TH, "g": U_G}[what])


def score_use_1(n, first):
    if first:
        return PER_G1 + (U_FIRST + n if n < NT else U_BEGIN + BEGIN.index(n))
    return PER_G1 + U_G1 + n + (n >= NT) + (n >= (NQ - 1) * NT)


def build(nc, x, out, w):
    with ExitStack() as ctx:
        def sb(name, shape, dt=F32):
            return ctx.enter_context(nc.sbuf_tensor(name, shape, dt))

        def sem(name):
            return ctx.enter_context(nc.semaphore(name))

        slot = [ctx.enter_context(nc.psum_tensor(f"score_slot{i}", [P, QW], F32)) for i in range(2)]
        pair = [ctx.enter_context(nc.psum_tensor(f"bank_pair{i}", [P, QW], F32)) for i in range(2)]
        t_bank = [pair[0][:, i * N:(i + 1) * N] for i in range(2)]
        o_bank = [pair[1][:, i * N:(i + 1) * N] for i in range(2)]

        r = sb("operands_r", [P, 4 * L + 2 * N + PT_RING * 2 * N], F32R)
        kh, kl = r[:, 0:L], r[:, L:2 * L]
        vh, vl = r[:, 2 * L:3 * L], r[:, 3 * L:4 * L]
        o = 4 * L
        qh, ql = r[:, o:o + N], r[:, o + N:o + 2 * N]
        th, tn = qh, ql
        o += 2 * N
        pth = [r[:, o + i * 2 * N:o + i * 2 * N + N] for i in range(PT_RING)]
        ptl = [r[:, o + i * 2 * N + N:o + (i + 1) * 2 * N] for i in range(PT_RING)]
        phh, phl = kh, kl
        hlh = [r[:, 2 * L + i * 2 * QW:2 * L + i * 2 * QW + QW] for i in range(HL_RING)]
        hll = [r[:, 2 * L + i * 2 * QW + QW:2 * L + (i + 1) * 2 * QW] for i in range(HL_RING)]
        ghl = [r[:, o + i * N:o + (i + 1) * N].rearrange("p (t c) -> p t c", t=NT) for i in range(2)]

        f = sb("work", [P, NQ, NT, QW])
        xc = f[:, 0, :, :].rearrange("p t n -> p (t n)")
        p0 = [f[:, 1 + i, :, :] for i in range(2)]
        osb = f[:, 3, 0:2, :].rearrange("p t n -> p (t n)")
        wb = f[:, 3, 2:4, :].rearrange("p t n -> p (t n)")
        xr = sb("x_residual", [P, L + N])
        acc = sb("acc", [P, L])
        xs = sb("x_stage", [P, N])
        zeros = sb("zeros", [P, N])
        gsb = sb("g_rows", [P, NT * CI])
        gtmp = sb("g_weighted", [P, NS * CI])
        gwh = [sb(f"g_whole{i}", [P, NW, P]) for i in range(2)]

        ident, gmat, ones = sb("ident", [P, P]), sb("gmat", [P, P]), sb("ones", [P, P])
        identr = sb("identr", [P, P], F32R)
        wq, wqs, wk, wv, wo, wvo = [sb(n + "_sb", [P, P]) for n in ("wq", "wqs", "wk", "wv", "wo", "wvo")]
        wth, wph, wout = [sb(n, [P, P]) for n in ("wth_sb", "wph_sb", "wout_sb")]
        wg = sb("wg_sb", [P, CI])
        vec = sb("vec", [P, 16])
        gamma, beta, bq, bk, bv, bo, bth, bph, bout = [vec[:, i:i + 1] for i in range(9)]
        qb, kb, vb, zero, eps = [vec[:, i:i + 1] for i in range(9, 14)]
        gbrow, gbb = sb("gbrow_sb", [1, CI]), sb("gbb", [P, CI])

        bst, mv = sb("bst", [P, NG, 6]), sb("mv", [P, 2])
        gn = sb("gn", [P, 8])
        dmean, e2, std, rstd, gmean, gain = [gn[:, i:i + 1] for i in range(6)]
        st0 = sb("st0", [P, 8 * 16])
        nm_first, z_first = st0[:, 0:NT], st0[:, NT:2 * NT]
        nmg = st0[:, 16:32].rearrange("p (q t) -> p q t", q=NQ)
        zg = st0[:, 32:48].rearrange("p (q t) -> p q t", q=NQ)
        nmin, zsum, zrec = st0[:, 8:12], st0[:, 12:16], st0[:, 48:52]
        diff, efac = st0[:, 64:80], st0[:, 80:96]
        ez, wgt = st0[:, 96:112], st0[:, 112:128]
        whr = sb("w_hi", [P, 16], F32R)
        wlr = sb("w_lo", [P, 16], F32R)
        st1 = sb("st1", [P, 8 * 16])
        nm1 = st1[:, 0:16].rearrange("p (q t) -> p q t", q=NQ)
        z1 = st1[:, 16:32].rearrange("p (q t) -> p q t", q=NQ)
        nmin1, zsum1, zrec1 = st1[:, 32:36], st1[:, 36:40], st1[:, 40:44]
        diff1, efac1, ez1, wgt1 = [st1[:, 48 + 16 * i:64 + 16 * i].rearrange("p (q t) -> p q t", q=NQ)
                                   for i in range(4)]

        def qt(a):
            return a.rearrange("p (q t) -> p q t", q=NQ)

        def tq(a):
            return a.rearrange("p q t -> p t q")

        s_wl = sem("weights_loaded")
        s_const, s_setup_pe, s_setup = sem("constants"), sem("setup_products"), sem("setup_done")
        s_full = [sem(f"slot_full{i}") for i in range(2)]
        s_free = [sem(f"slot_free{i}") for i in range(2)]
        s_pair_full = [sem(f"pair_full{i}") for i in range(2)]
        s_pair_free = [sem(f"pair_free{i}") for i in range(2)]
        s_x = [sem(f"x_loaded{i}") for i in range(NQ)]
        s_bs, s_mv, s_gm, s_dm, s_e2, s_std, s_rstd, s_gain = [
            sem(n) for n in ("chunk_stats", "channel_stats", "group_mean", "mean_offset", "second_moment",
                             "std", "rstd", "gain")]
        s_xr, s_xb, s_xn = sem("residual_loaded"), sem("residual_biased"), sem("x_normalised")
        s_gm2, s_gmc = sem("group_second_moment"), sem("group_mean_copied")
        s_ph = sem("projection_hi")
        s_qhi = sem("q_hi")
        s_max, s_cp = sem("max0"), sem("first_quarter_stats")
        s_t = [sem(f"transposed{i}") for i in range(2)]
        s_hi = sem("pt_hi")
        s_lo = [sem(f"pt_lo{i}") for i in range(2)]
        s_pv = [sem(f"pv_done{i}") for i in range(PT_RING)]
        s_oev = [sem(f"sum_evacuated{i}") for i in range(2)]
        s_mn, s_df, s_e, s_ez, s_zs, s_zr, s_w, s_wh, s_wlo = [
            sem(n) for n in ("nmin0", "diff0", "efac0", "ez0", "zsum0", "zrec0", "wgt0", "w_hi0", "w_lo0")]
        s_wb = sem("weights_broadcast")
        s_pr, s_h1, s_h2, s_x1 = sem("weighted"), sem("half_sum"), sem("quarter_sum"), sem("x1_group")
        s_phi = sem("phi_hi")
        s_thh, s_th, s_xs, s_gs = sem("theta_hi"), sem("theta_staged"), sem("x_staged"), sem("g_rows_ready")
        s_az = sem("acc_zeroed")
        s_max1, s_hi1, s_lo1 = sem("max1"), sem("p1_hi"), sem("p1_lo")
        s_mn1, s_df1, s_e1, s_ez1, s_zs1, s_zr1, s_w1 = [
            [sem(f"{n}_{half}") for half in ("whole", "split")]
            for n in ("nmin1", "diff1", "efac1", "ez1", "zsum1", "zrec1", "wgt1")]
        s_gw, s_gt, s_gh, s_g = sem("g_whole_ready"), sem("g_weighted"), sem("g_hi"), sem("g_ready")
        s_masks = sem("masks_ready")
        s_pvs = [sem(f"pv1_split{i}") for i in range(HL_RING)]
        s_pvf = sem("pv1_whole")
        s_acc = [sem(f"acc_added{i}") for i in range(2)]
        s_out = sem("stored")

        class Groups:

            def __init__(self, eng, b, g, groups):
                self.eng, self.made = eng, {}
                self.run, self.off = (b * groups, g) if isinstance(g, int) else (b * groups + g, 0)

            def __call__(self, k, n):
                if k not in self.made:
                    self.made[k] = self.eng.snap(self.run * k)
                return self.made[k] + (self.off * k + n)

        class Uses:

            def __init__(self, eng, b, g=0, per=0):
                fixed = isinstance(g, int)
                run = b * (USES // 2) if fixed else b * (USES // 2) + g * (per // 2)
                self.base = run if isinstance(run, int) else eng.snap(run)
                self.off = g * (per // 2) if fixed else 0

            def before(self, u):
                return self.base + (CREDIT + self.off + u // 2)

            def done(self, u):
                return self.base + (self.off + u // 2 + 1)

        class Home:

            def __init__(self, uses, b, n, first):
                if first and n >= NT and n % 2:
                    k, i = divmod((n - NT) // 2, 2)
                    self.bank, self.s_full, self.s_free = pair[i], s_pair_full[i], s_pair_free[i]
                    self.filled = self.given_up = b * PAIR_USES + k + 1
                    self.before = b * PAIR_USES + k if k else None
                else:
                    u = score_use_1(n, first)
                    self.bank, self.s_full, self.s_free = slot[u % 2], s_full[u % 2], s_free[u % 2]
                    self.filled, self.before, self.given_up = uses.done(u), uses.before(u), uses.before(u) + 1

        def wait_full(eng, uses, u):
            eng.wait_ge(s_full[u % 2], uses.done(u))

        def wait_given_up(eng, uses, u):
            eng.wait_ge(s_free[u % 2], uses.before(u) + 1)

        def pool_copy(dst, src, n):
            return nc.gpsimd.tensor_tensor(dst, src, n, ALU.add)

        block = ctx.enter_context(nc.Block())

        @block.sync
        def _(sp):
            for s in (*s_free, *s_lo, *s_oev, *s_pv, *s_t, *s_pvs, *s_acc, s_pr, s_h1, s_h2):
                sp.sem_inc(s, CREDIT)
            sp.sem_inc(s_out, 16 * CREDIT)
            for dst, src in w:
                tile = {"wq": wq, "wk": wk, "wv": wv, "wo": wo, "wg": wg, "gbrow": gbrow, "gamma": gamma,
                        "beta": beta, "bq": bq, "bk": bk, "bv": bv, "bo": bo, "bout": bout,
                        "wth0": wth[:, 0:CI], "wth1": wth[:, CI:P], "wph0": wph[:, 0:CI], "wph1": wph[:, CI:P],
                        "wout0": wout[0:CI, :], "wout1": wout[CI:P, :],
                        "bth0": vec[0:CI, 6:7], "bth1": vec[CI:P, 6:7],
                        "bph0": vec[0:CI, 7:8], "bph1": vec[CI:P, 7:8]}[dst]
                sp.dma_start(tile[:, :] if hasattr(tile, "name") else tile, src).then_inc(s_wl, 16)

            def load(b):
                for c in range(NQ):
                    sp.dma_start(xc[:, c * QW:(c + 1) * QW], x[b, :, c * QW:(c + 1) * QW]).then_inc(s_x[c], 16)

            def store(b):
                uses = Uses(sp, b)
                for c in range(NQ):
                    wait_given_up(sp, uses, out_use(c))
                    sp.dma_start(out[b, :, c * QW:(c + 1) * QW], xr[:, c * QW:(c + 1) * QW]).then_inc(s_out, 16)

            def load_residual(b):
                sp.dma_start(xr[:, 0:L], x[b, :, :]).then_inc(s_xr, 16)

            def end_of_batch(b, following):
                sp.wait_ge(s_pvs[NS - 1], b * (NG * NQ * NS // HL_RING) + (NG - 1) * (NQ * NS // HL_RING) + 1 + CREDIT)
                load(following)
                store(b)

            load(0)
            load_residual(0)
            with sp.Fori(0, B - 1) as b:
                end_of_batch(b, b + 1)
                sp.wait_ge(s_out, b * (16 * NQ) + 16 * (NQ + CREDIT))
                load_residual(b + 1)
            end_of_batch(B - 1, 0)
            sp.wait_ge(s_out, 16 * (NQ * B + CREDIT))

        @block.tensor
        def _(pe):
            mm = pe.matmul
            pe.wait_ge(s_wl, 16 * len(w))
            pe.wait_ge(s_const, 4)
            mm(pair[0][:, 0:P], wv[:, :], wo[:, :], start=True, stop=True)
            mm(pair[1][:, 0:1], wq[:, :], beta, start=True, stop=True)
            mm(pair[1][:, 1:2], wk[:, :], beta, start=True, stop=True)
            mm(pair[1][:, 2:2 + CI], ones[0:1, :], gbrow[:, :], start=True, stop=True).then_inc(s_setup_pe, 1)
            pe.wait_ge(s_setup, 1)
            mm(pair[0][:, N:N + 1], wvo[:, :], beta, start=True, stop=False)
            mm(pair[0][:, N:N + 1], wo[:, :], bv, start=False, stop=True).then_inc(s_setup_pe, 1)
            pe.wait_ge(s_setup, 2)

            def scores_0(uses, u, q, t):
                pe.wait_ge(s_free[u % 2], uses.before(u))
                s = slot[u % 2]
                for a, kk, first, last in ((qh, kh, True, False), (qh, kl, False, False), (ql, kh, False, True)):
                    for c in range(2):
                        ins = mm(s[:, c * N:(c + 1) * N], a[:, t * P:(t + 1) * P],
                                 kk[:, q * QW + c * N:q * QW + (c + 1) * N], start=first, stop=last)
                ins.then_inc(s_full[u % 2], 1)

            def qproj(uses, u, cols):
                pe.wait_ge(s_free[u % 2], uses.before(u))
                mm(slot[u % 2][:, 0:N], wqs[:, :], cols, start=True, stop=True).then_inc(s_full[u % 2], 1)

            def group_0(b, g, last):
                uses = Uses(pe, b, g, PER_G0)
                gi = Groups(pe, b, g, NG)

                def transpose(n):
                    if n % MT == 0:
                        u = U_G0 + score_use_0(n // MT - 1, 0) if n else PREV_S
                        wait_given_up(pe, uses, u + NT - 2)
                        wait_given_up(pe, uses, u + NT - 1)
                    pe.wait_ge(s_lo[n % 2], gi(NM // 2, CREDIT + n // 2))
                    for t in range(NT):
                        ins = pe.transpose(t_bank[n % 2][:, t * P:(t + 1) * P],
                                           p0[(n // MT) % 2][:, t, (n % MT) * P:(n % MT + 1) * P], ident[:, :])
                    ins.then_inc(s_t[n % 2], 1)

                def pv(n):
                    q, j = n // MT, n % MT
                    if j == 0:
                        pe.wait_ge(s_oev[q % 2], gi(2, CREDIT + q // 2))
                    pe.wait_ge(s_lo[n % 2], gi(NM // 2, CREDIT + n // 2 + 1))
                    ob, c = o_bank[q % 2], slice(n * P, (n + 1) * P)
                    mm(ob, vh[:, c], pth[n % PT_RING], start=(j == 0), stop=False)
                    mm(ob, vl[:, c], pth[n % PT_RING], start=False, stop=False)
                    mm(ob, vh[:, c], ptl[n % PT_RING], start=False, stop=(j == MT - 1)).then_inc(
                        s_pv[n % PT_RING], 1)

                def weights(j):
                    u = U_G0 + w_use(j, last)
                    if j == 0:
                        pe.wait_ge(s_wlo, gi(1, 1))
                    pe.wait_ge(s_free[u % 2], uses.before(u))
                    for i, q in enumerate(((0, 1), (2,), (3,))[j]):
                        for t in range(NT):
                            dst = slot[u % 2][:, i * N + t * P:i * N + (t + 1) * P]
                            k = q * NT + t
                            mm(dst, whr[:, k:k + 1].broadcast_to([P, P]), identr[:, :], start=True, stop=False)
                            ins = mm(dst, wlr[:, k:k + 1].broadcast_to([P, P]), identr[:, :], start=False, stop=True)
                    ins.then_inc(s_full[u % 2], 1)

                for n in range(NM):
                    q, j = n // MT, n % MT
                    transpose(n)
                    if j in SCORES_AT and not (last and q == NQ - 1):
                        t = SCORES_AT[j]
                        if q == NQ - 1 and t == 0:
                            wait_given_up(pe, uses, U_G0 + U_QPROJ)
                        scores_0(uses, U_G0 + score_use_0(q, t), (q + 1) % NQ, t)
                    if q == NQ - 2 and j == 6 and not last:
                        qproj(uses, U_G0 + U_QPROJ, xc[:, bass.ts(g + 1, N)])
                    if last and (q, j) in FIRST_1:
                        t = FIRST_1[q, j]
                        if t == "phi":
                            phi(b, 0)
                        elif t == "theta":
                            theta_first(b)
                        else:
                            if t == 0:
                                wait_given_up(pe, Uses(pe, b), U_PHI0)
                                wait_given_up(pe, Uses(pe, b), U_TH0)
                            scores_1(Home(Uses(pe, b, -1, PER_G1), b, t, True), t)
                    if q == NQ - 1 and j >= 6:
                        weights(j - 6)
                    if n >= PV_LAG:
                        pv(n - PV_LAG)
                pv(NM - 2)
                weights(2)
                pv(NM - 1)

            def scores_1(home, n):
                q, t = n // NT, n % NT
                if home.before is not None:
                    pe.wait_ge(home.s_free, home.before)
                for ph, first in ((phh, True), (phl, False)):
                    for c in range(2):
                        ins = mm(home.bank[:, c * N:(c + 1) * N], th[:, t * P:(t + 1) * P],
                                 ph[:, q * QW + c * N:q * QW + (c + 1) * N], start=first, stop=not first)
                ins.then_inc(home.s_full, 1)

            def phi(b, c):
                uses, u = Uses(pe, b), phi_use(c)
                pe.wait_ge(s_x1, b * NG + (c + 1) * (QW // N))
                pe.wait_ge(s_free[u % 2], uses.before(u))
                for i in range(2):
                    ins = mm(slot[u % 2][:, i * N:(i + 1) * N], wph[:, :],
                             xr[:, c * QW + i * N:c * QW + (i + 1) * N], start=True, stop=True)
                ins.then_inc(s_full[u % 2], 1)

            def theta_first(b):
                uses = Uses(pe, b)
                pe.wait_ge(s_free[U_TH0 % 2], uses.before(U_TH0))
                mm(slot[U_TH0 % 2][:, 0:N], wth[:, :], xr[:, 0:N], start=True, stop=True).then_inc(
                    s_full[U_TH0 % 2], 1)

            def iteration_1(b, g, has_pv, has_scores):
                first_run = not has_pv
                uses = Uses(pe, b, g, PER_G1)
                gi = Groups(pe, b, g, NG)

                def scores(n):
                    if n < NT:
                        pe.wait_ge(s_th, gi(NT, n + 1))
                    home = Home(uses, b, n, first_run)
                    if home.before is None:
                        for i in range(2):
                            pe.wait_ge(s_oev[i], b * (2 * NG) + 2 * NG + CREDIT)
                    scores_1(home, n)

                def theta():
                    u = use_1("theta", first_run)
                    pe.wait_ge(s_free[u % 2], uses.before(u))
                    mm(slot[u % 2][:, 0:N], wth[:, :], xr[:, bass.ds(g * N + 2 * N, N)],
                       start=True, stop=True).then_inc(s_full[u % 2], 1)

                def grows():
                    u = use_1("g", first_run)
                    pe.wait_ge(s_xs, gi(1, 2))
                    pe.wait_ge(s_free[u % 2], uses.before(u))
                    for t in range(NT):
                        ins = mm(slot[u % 2][:, t * CI:(t + 1) * CI], xs[:, t * P:(t + 1) * P], wg[:, :],
                                 start=True, stop=True)
                    ins.then_inc(s_full[u % 2], 1)

                def pv(n):
                    q, t = n // NT, n % NT
                    a = pair[q % 2]
                    if t == 0:
                        pe.wait_ge(s_acc[q % 2], gi(2, CREDIT + q // 2))
                    if t in WHOLE:
                        i = WHOLE.index(t)
                        pe.wait_ge(s_gw, gi(NQ * NW, q * NW + i + 1))
                        for c in range(2):
                            ins = mm(a[:, c * N:(c + 1) * N], gwh[q % 2][:, i, :],
                                     f[:, q, t, c * N:(c + 1) * N], start=(t == 0), stop=False)
                        ins.then_inc(s_pvf, 1)
                    else:
                        i = SPLIT.index(t)
                        m = q * NS + i
                        pe.wait_ge(s_g, gi(NQ * NS, m + 1))
                        pe.wait_ge(s_lo1, gi(NQ * NS, m + 1))
                        for part in (hlh, hll):
                            for c in range(2):
                                ins = mm(a[:, c * N:(c + 1) * N], ghl[q % 2][:, i, :],
                                         part[m % HL_RING][:, c * N:(c + 1) * N],
                                         start=False, stop=(t == NT - 1 and part is hll))
                        ins.then_inc(s_pvs[m % HL_RING], 1)

                for q in range(1 if first_run else 0, NQ):
                    if first_run and q == NQ - 2:
                        phi(b, NQ - 1)
                    ns = np_ = 0
                    for what in PE_ORDER[q]:
                        if what == "P" and has_pv:
                            pv(q * NT + np_)
                            np_ += 1
                        if what == "T" and has_scores:
                            theta()
                        if what == "G" and has_scores:
                            grows()
                        if what == "S" and has_scores:
                            scores(q * NT + ns)
                            ns += 1
                        if not has_scores and q == NQ - 1 and what == "P" and np_ == 2:
                            group_mean(b + 1, slot[U_STATS % 2], Uses(pe, b))
                    if not has_scores and q == NQ - 1:
                        group_second_moment(b + 1, slot[U_STATS % 2], s_full[U_STATS % 2])
                    if not has_scores and q > 0:
                        project_out(b, q - 1)

            def project_out(b, c):
                uses = Uses(pe, b)
                u = out_use(c)
                pe.wait_ge(s_acc[c % 2], b * (NG * 2) + (NG - 1) * 2 + c // 2 + 1 + CREDIT)
                pe.wait_ge(s_free[u % 2], uses.before(u))
                for i in range(2):
                    ins = mm(slot[u % 2][:, i * N:(i + 1) * N], wout[:, :],
                             acc[:, c * QW + i * N:c * QW + (i + 1) * N], start=True, stop=True)
                ins.then_inc(s_full[u % 2], 1)

            def group_mean(b, bank, uses):
                pe.wait_ge(s_mv, b + 1)
                if uses:
                    pe.wait_ge(s_free[U_STATS % 2], uses.before(U_STATS))
                mm(bank[:, 0:1], gmat[:, :], mv[:, 0:1], start=True, stop=True).then_inc(s_gm, 1)

            def group_second_moment(b, bank, done):
                pe.wait_ge(s_e2, b + 1)
                mm(bank[:, N:N + 1], gmat[:, :], e2, start=True, stop=True).then_inc(done, 1)

            group_mean(0, pair[0], None)
            group_second_moment(0, pair[0], s_gm2)
            with pe.Fori(0, B) as b:
                uses = Uses(pe, b)

                def project(u, c, is_k):
                    pe.wait_ge(s_xn, b * NQ + c + 1)
                    pe.wait_ge(s_free[u % 2], uses.before(u))
                    if is_k:
                        for i in range(2):
                            ins = mm(slot[u % 2][:, i * N:(i + 1) * N], wk[:, :],
                                     xc[:, c * QW + i * N:c * QW + (i + 1) * N], start=True, stop=True)
                    else:
                        for i in range(MT):
                            ins = mm(slot[u % 2][:, i * P:(i + 1) * P], xc[:, c * QW + i * P:c * QW + (i + 1) * P],
                                     wvo[:, :], start=True, stop=True)
                    ins.then_inc(s_full[u % 2], 1)

                for c in range(NQ):
                    project(U_PROJ + c, c, True)
                project(U_PROJ + NQ, 0, False)
                qproj(uses, U_Q0, xc[:, 0:N])
                wait_given_up(pe, uses, U_Q0)
                for t in range(NT):
                    scores_0(uses, U_S0 + t, 0, t)
                for c in range(1, NQ):
                    project(U_V + c - 1, c, False)
                with pe.Fori(0, NG - 1) as g:
                    group_0(b, g, False)
                group_0(b, NG - 1, True)

                phi(b, 1)
                phi(b, 2)
                iteration_1(b, -1, False, True)
                with pe.Fori(0, NG - 1) as g:
                    iteration_1(b, g, True, True)
                iteration_1(b, NG - 1, True, False)
                project_out(b, NQ - 1)

        @block.scalar
        def _(act):
            def exp0(uses, u, t, nm, z, dst):
                act.activation(dst, slot[u % 2][:, :], ACT.Exp, bias=nm, accum_out=z).then_inc(s_free[u % 2], 1)

            def phi_hi(b, c):
                u = phi_use(c)
                wait_full(act, Uses(act, b), u)
                act.activation(phh[:, c * QW:(c + 1) * QW], slot[u % 2][:, :], ACT.Identity,
                               bias=bph).then_inc(s_phi, 1)

            def exp_1(home, n):
                q, t = n // NT, n % NT
                act.activation(f[:, q, t, :], home.bank[:, :], ACT.Exp, bias=nm1[:, q, t:t + 1],
                               accum_out=z1[:, q, t:t + 1]).then_inc(home.s_free, 1)

            def group_0(b, g, last):
                uses = Uses(act, b, g, PER_G0)
                gi = Groups(act, b, g, NG)

                def hi(n):
                    act.wait_ge(s_t[n % 2], gi(NM // 2, CREDIT + n // 2 + 1))
                    act.wait_ge(s_pv[n % PT_RING], gi(NM // PT_RING, CREDIT + n // PT_RING))
                    act.activation(pth[n % PT_RING], t_bank[n % 2], ACT.Copy).then_inc(s_hi, 1)

                def sum_out(q):
                    n = q * MT + MT - 1
                    act.wait_ge(s_h1, gi(1, CREDIT + 0))
                    act.wait_ge(s_pv[n % PT_RING], gi(NM // PT_RING, CREDIT + n // PT_RING + 1))
                    act.activation(osb[:, q * N:(q + 1) * N], o_bank[q % 2], ACT.Copy).then_inc(s_oev[q % 2], 1)

                def weights_out(j):
                    u = U_G0 + w_use(j, last)
                    wait_full(act, uses, u)
                    act.wait_ge(s_h2, gi(1, CREDIT + 0))
                    n0, n1 = ((0, 2), (2, 3), (3, 4))[j]
                    act.activation(wb[:, n0 * N:n1 * N], slot[u % 2][:, 0:(n1 - n0) * N], ACT.Copy).then_inc(
                        s_free[u % 2], 1)

                for n in range(NM):
                    q, j = n // MT, n % MT
                    hi(n)
                    if q == NQ - 2 and j == 6 and not last:
                        wait_full(act, uses, U_G0 + U_QPROJ)
                        act.activation(qh, slot[(U_G0 + U_QPROJ) % 2][:, 0:N], ACT.Identity, bias=qb).then_inc(
                            s_qhi, 1)
                    if last and FIRST_1.get((q, j)) == "phi":
                        phi_hi(b, 0)
                    if last and FIRST_1.get((q, j)) == "theta":
                        wait_full(act, Uses(act, b), U_TH0)
                        act.activation(th, slot[U_TH0 % 2][:, 0:N], ACT.Identity, bias=bth).then_inc(s_thh, 1)
                    if last and (q, j) in FIRST_EXP_1:
                        t = FIRST_EXP_1[q, j]
                        act.wait_ge(s_max1, b * (NG * NQ * NT) + t + 1)
                        exp_1(Home(Uses(act, b, -1, PER_G1), b, t, True), t)
                    if j in EXP_AT and not (last and q == NQ - 1):
                        t = EXP_AT[j]
                        u = U_G0 + score_use_0(q, t)
                        act.wait_ge(s_max, gi(NQ * NT, NT * (q + 1) + t + 1))
                        if t == 0:
                            act.wait_ge(s_t[1], gi(NM // 2, CREDIT + q * (MT // 2)))
                        if q == NQ - 1:
                            exp0(uses, u, t, nm_first[:, t:t + 1], z_first[:, t:t + 1], p0[0][:, t, :])
                        else:
                            exp0(uses, u, t, nmg[:, q + 1, t:t + 1], zg[:, q + 1, t:t + 1], p0[(q + 1) % 2][:, t, :])
                    if q == NQ - 1 and j == 2:
                        act.wait_ge(s_df, gi(1, 1))
                        act.activation(efac, diff, ACT.Exp).then_inc(s_e, 1)
                    if j == PV_LAG + 1 and q > 0:
                        sum_out(q - 1)
                weights_out(0)
                weights_out(1)
                weights_out(2)
                sum_out(NQ - 1)

            def iteration_1(b, g, has_pv, has_scores):
                first_run = not has_pv
                uses = Uses(act, b, g, PER_G1)
                gi = Groups(act, b, g, NG)

                def hi(n):
                    q, t = n // NT, n % NT
                    if q == NQ:
                        home = Home(uses, b, t, first_run)
                        act.wait_ge(home.s_free, home.given_up)
                    m = q * NS + SPLIT.index(t)
                    act.wait_ge(s_pvs[m % HL_RING], gi(NQ * NS // HL_RING, CREDIT + m // HL_RING))
                    act.activation(hlh[m % HL_RING], f[:, q % NQ, t, :], ACT.Copy).then_inc(s_hi1, 1)

                def theta_hi():
                    u = use_1("theta", first_run)
                    wait_full(act, uses, u)
                    if has_pv:
                        act.wait_ge(s_th, gi(NT, NT))
                    act.activation(tn, slot[u % 2][:, 0:N], ACT.Identity, bias=bth).then_inc(s_thh, 1)

                def exp1(n):
                    q, t = n // NT, n % NT
                    act.wait_ge(s_max1, gi(NQ * NT, NQ * NT + n + 1))
                    if has_pv and t in WHOLE:
                        act.wait_ge(s_pvf, gi(NQ * NW, q * NW + WHOLE.index(t) + 1))
                    elif has_pv:
                        act.wait_ge(s_lo1, gi(NQ * NS, q * NS + SPLIT.index(t) + 1))
                    exp_1(Home(uses, b, n, first_run), n)

                def efac(h):
                    act.wait_ge(s_df1[h], gi(1, 2))
                    act.activation(efac1[:, :, HALVES[h]], diff1[:, :, HALVES[h]], ACT.Exp).then_inc(s_e1[h], 1)

                for q in range(1 if first_run else 0, NQ):
                    if first_run and q == NQ - 2:
                        phi_hi(b, NQ - 1)
                    for what in ACT_ORDER[q]:
                        kind, i = what[0], int(what[1])
                        if kind == "H" and (has_pv if q * NT + i < NQ * NT else has_scores):
                            hi(q * NT + i)
                        if kind == "T" and has_scores:
                            theta_hi()
                        if kind == "E" and has_scores:
                            exp1(q * NT + i)
                        if kind == "D" and has_scores:
                            efac(i)

            def root(bank):
                act.activation(std, bank[:, N:N + 1], ACT.Sqrt, bias=eps).then_inc(s_std, 1)
                act.activation(gn[:, 7:8], zero, ACT.Exp)

            act.wait_ge(s_setup, 2)
            act.wait_ge(s_gm2, 1)
            root(pair[0])
            with act.Fori(0, B) as b:
                uses = Uses(act, b)

                def high(u, dst, bias):
                    wait_full(act, uses, u)
                    act.activation(dst, slot[u % 2][:, :], ACT.Identity, bias=bias).then_inc(s_ph, 1)

                for c in range(NQ):
                    high(U_PROJ + c, kh[:, c * QW:(c + 1) * QW], kb)
                high(U_PROJ + NQ, vh[:, 0:QW], zero)
                wait_full(act, uses, U_Q0)
                act.activation(qh, slot[U_Q0 % 2][:, 0:N], ACT.Identity, bias=qb).then_inc(s_qhi, 1)
                for t in range(NT):
                    act.wait_ge(s_max, b * (NG * NQ * NT) + t + 1)
                    exp0(uses, U_S0 + t, t, nm_first[:, t:t + 1], z_first[:, t:t + 1], p0[0][:, t, :])
                for c in range(1, NQ):
                    high(U_V + c - 1, vh[:, c * QW:(c + 1) * QW], zero)
                with act.Fori(0, NG - 1) as g:
                    group_0(b, g, False)
                group_0(b, NG - 1, True)

                phi_hi(b, 1)
                phi_hi(b, 2)
                iteration_1(b, -1, False, True)
                with act.Fori(0, NG - 1) as g:
                    iteration_1(b, g, True, True)
                iteration_1(b, NG - 1, True, False)
                wait_full(act, uses, U_STATS)
                root(slot[U_STATS % 2])

        @block.vector
        def _(dve):
            def minus(dst, src, bias, high):
                return dve.scalar_tensor_tensor(out=dst, in0=src, scalar=bias, in1=high.bitcast(F32),
                                                op0=ALU.add, op1=ALU.subtract)

            dve.memset(zero, 0.0)
            dve.memset(eps, EPS)
            dve.memset(xr[:, L:L + N], 0.0).then_inc(s_const, 1)
            dve.wait_ge(s_const, 4)
            dve.tensor_copy(identr[:, :], ident[:, :])
            dve.wait_ge(s_wl, 16 * len(w))
            dve.tensor_scalar(wqs[:, :], wq[:, :], SCALE, None, ALU.mult)
            dve.wait_ge(s_setup_pe, 1)
            dve.tensor_copy(wvo[:, :], pair[0][:, 0:P]).then_inc(s_setup, 1)
            dve.tensor_scalar(qb, pair[1][:, 0:1], bq, SCALE, ALU.add, ALU.mult)
            dve.tensor_tensor(kb, pair[1][:, 1:2], bk, ALU.add)
            dve.tensor_copy(gbb[:, :], pair[1][:, 2:2 + CI])
            dve.wait_ge(s_setup_pe, 2)
            dve.tensor_tensor(vb, pair[0][:, N:N + 1], bo, ALU.add).then_inc(s_setup, 1)

            def softmax_weights(i, nm, z, nmn, df, e, ezt, zs, zr, wt, s):
                s_mn_, s_df_, s_e_, s_ez_, s_zs_, s_zr_, s_w_ = s
                if df is not None:
                    dve.tensor_reduce(nmn, tq(nm), AXX, ALU.min).then_inc(s_mn_, 1)
                    dve.wait_ge(s_mn_, i(1, 1))
                    dve.tensor_tensor(qt(df), nmn.unsqueeze(1).broadcast_to([P, NQ, NT]), nm,
                                      ALU.subtract).then_inc(s_df_, 1)
                if e is not None:
                    dve.wait_ge(s_e_, i(1, 1))
                    dve.tensor_tensor(qt(ezt), qt(e), z, ALU.mult).then_inc(s_ez_, 1)
                    dve.wait_ge(s_ez_, i(1, 1))
                    dve.tensor_reduce(zs, tq(qt(ezt)), AXX, ALU.add).then_inc(s_zs_, 1)
                    dve.wait_ge(s_zs_, i(1, 1))
                    dve.reciprocal(zr, zs).then_inc(s_zr_, 1)
                    dve.wait_ge(s_zr_, i(1, 1))
                    dve.tensor_tensor(qt(wt), qt(e), zr.unsqueeze(1).broadcast_to([P, NQ, NT]),
                                      ALU.mult).then_inc(s_w_, 1)

            def phi_lo(b, c):
                u, cols = phi_use(c), slice(c * QW, (c + 1) * QW)
                dve.wait_ge(s_phi, b * NQ + c + 1)
                minus(phl[:, cols], slot[u % 2][:, :], bph, phh[:, cols]).then_inc(s_free[u % 2], 1)

            def maximum_1(home, n):
                q, t = n // NT, n % NT
                dve.wait_ge(home.s_full, home.filled)
                dve.tensor_reduce(nm1[:, q, t:t + 1], home.bank[:, :], AXX, ALU.max, negate=True).then_inc(s_max1, 1)

            def group_0(b, g, last):
                uses = Uses(dve, b, g, PER_G0)
                gi = Groups(dve, b, g, NG)
                chain = (s_mn, s_df, s_e, s_ez, s_zs, s_zr, s_w)

                def lo(n):
                    dve.wait_ge(s_hi, gi(NM, n + 1))
                    dve.tensor_tensor(ptl[n % PT_RING], t_bank[n % 2], pth[n % PT_RING].bitcast(F32),
                                      ALU.subtract).then_inc(s_lo[n % 2], 1)

                for n in range(NM):
                    q, j = n // MT, n % MT
                    lo(n)
                    if q == NQ - 2 and j == 6 and not last:
                        dve.wait_ge(s_qhi, gi(1, 2))
                        u = U_G0 + U_QPROJ
                        minus(ql, slot[u % 2][:, 0:N], qb, qh).then_inc(s_free[u % 2], 1)
                    if last and (q, j) in FIRST_1:
                        t = FIRST_1[q, j]
                        if t == "phi":
                            phi_lo(b, 0)
                        elif t == "theta":
                            dve.wait_ge(s_thh, b * (NG + 1) + 1)
                            minus(th[CI:P, :], slot[U_TH0 % 2][CI:P, 0:N], bth[CI:P, :], th[CI:P, :]).then_inc(
                                s_free[U_TH0 % 2], 1)
                        else:
                            maximum_1(Home(Uses(dve, b, -1, PER_G1), b, t, True), t)
                    if j in SCORES_AT and not (last and q == NQ - 1):
                        t = SCORES_AT[j]
                        u = U_G0 + score_use_0(q, t)
                        wait_full(dve, uses, u)
                        dst = nm_first[:, t:t + 1] if q == NQ - 1 else nmg[:, q + 1, t:t + 1]
                        dve.tensor_reduce(dst, slot[u % 2][:, :], AXX, ALU.max, negate=True).then_inc(s_max, 1)
                    if q == 0 and j == 1:
                        wait_given_up(dve, uses, PREV_S + NT - 2)
                        wait_given_up(dve, uses, PREV_S + NT - 1)
                        dve.tensor_copy(nmg[:, 0, :], nm_first).then_inc(s_cp, 1)
                        dve.tensor_copy(zg[:, 0, :], z_first).then_inc(s_cp, 1)
                    if q == NQ - 1 and j == 1:
                        u = U_G0 + score_use_0(NQ - 2, NT - 1)
                        wait_given_up(dve, uses, u - 1)
                        wait_given_up(dve, uses, u)
                        dve.wait_ge(s_cp, gi(2, 2))
                        softmax_weights(gi, nmg, zg, nmin, diff, None, None, None, None, None, chain)
                    if q == NQ - 1 and j == 3:
                        softmax_weights(gi, None, zg, None, None, efac, ez, zsum, zrec, wgt, chain)
                        dve.wait_ge(s_w, gi(1, 1))
                        dve.wait_ge(s_pr, gi(1, CREDIT + 0))
                        dve.tensor_copy(whr[:, :], wgt).then_inc(s_wh, 1)
                        dve.wait_ge(s_wh, gi(1, 1))
                        dve.tensor_tensor(wlr[:, :], wgt, whr[:, :].bitcast(F32), ALU.subtract).then_inc(s_wlo, 1)

            def iteration_1(b, g, has_pv, has_scores):
                first_run = not has_pv
                uses = Uses(dve, b, g, PER_G1)
                gi, gth = Groups(dve, b, g, NG), Groups(dve, b, g, NG + 1)

                nxt = Groups(dve, b, g + 1, NG)

                def add_sum(q):
                    m = q * NS + NS - 1
                    dve.wait_ge(s_pvs[m % HL_RING], gi(NQ * NS // HL_RING, CREDIT + m // HL_RING + 1))
                    dve.wait_ge(s_acc[q % 2], gi(2, CREDIT + q // 2))
                    dve.tensor_tensor(acc[:, q * QW:(q + 1) * QW], pair[q % 2][:, :], acc[:, q * QW:(q + 1) * QW],
                                      ALU.add).then_inc(s_acc[q % 2], 1)

                def lo(n):
                    q, t = n // NT, n % NT
                    m = q * NS + SPLIT.index(t)
                    dve.wait_ge(s_hi1, gi(NQ * NS, m + 1))
                    dve.tensor_tensor(hll[m % HL_RING], f[:, q % NQ, t, :], hlh[m % HL_RING].bitcast(F32),
                                      ALU.subtract).then_inc(s_lo1, 1)

                def theta_lo():
                    u = use_1("theta", first_run)
                    dve.wait_ge(s_thh, gth(1, 3))
                    minus(tn[CI:P, :], slot[u % 2][CI:P, 0:N], bth[CI:P, :], tn[CI:P, :]).then_inc(s_free[u % 2], 1)

                def g_rows():
                    u = use_1("g", first_run)
                    wait_full(dve, uses, u)
                    if has_pv:
                        dve.wait_ge(s_g, gi(NQ * NS, NQ * NS))
                    dve.tensor_tensor(gsb[:, :].rearrange("p (t c) -> p t c", t=NT),
                                      slot[u % 2][:, 0:NT * CI].rearrange("p (t c) -> p t c", t=NT),
                                      gbb[:, :].unsqueeze(1).broadcast_to([P, NT, CI]),
                                      ALU.add).then_inc(s_free[u % 2], 1)

                def offsets(h):
                    c = HALVES[h]
                    dve.wait_ge(s_max1, gi(NQ * NT, NQ * NT + (NQ - 1) * NT + c.stop))
                    dve.tensor_reduce(nmin1[:, c], nm1[:, :, c].rearrange("p q t -> p t q"), AXX, ALU.min).then_inc(
                        s_mn1[h], 1)
                    dve.wait_ge(s_mn1[h], nxt(1, 1))
                    dve.tensor_tensor(diff1[:, :, c], nmin1[:, c].unsqueeze(1).broadcast_to([P, NQ, 2]), nm1[:, :, c],
                                      ALU.subtract).then_inc(s_df1[h], 1)

                def row_sums(h):
                    c = HALVES[h]
                    for t in range(c.start, c.stop):
                        home = Home(uses, b, (NQ - 1) * NT + t, first_run)
                        dve.wait_ge(home.s_free, home.given_up)
                    dve.wait_ge(s_e1[h], nxt(1, 1))
                    dve.tensor_tensor(ez1[:, :, c], efac1[:, :, c], z1[:, :, c], ALU.mult).then_inc(s_ez1[h], 1)
                    dve.wait_ge(s_ez1[h], nxt(1, 1))
                    dve.tensor_reduce(zsum1[:, c], ez1[:, :, c].rearrange("p q t -> p t q"), AXX, ALU.add).then_inc(
                        s_zs1[h], 1)

                def weights_1(h):
                    c = HALVES[h]
                    dve.wait_ge(s_zs1[h], nxt(1, 1))
                    dve.reciprocal(zrec1[:, c], zsum1[:, c]).then_inc(s_zr1[h], 1)
                    dve.wait_ge(s_zr1[h], nxt(1, 1))
                    dve.tensor_tensor(wgt1[:, :, c], efac1[:, :, c], zrec1[:, c].unsqueeze(1).broadcast_to([P, NQ, 2]),
                                      ALU.mult).then_inc(s_w1[h], 1)

                for q in range(1 if first_run else 0, NQ):
                    if first_run and q == NQ - 2:
                        phi_lo(b, NQ - 1)
                    for what in DVE_ORDER[q]:
                        kind, i = what[0], q * NT + int(what[1])
                        if kind == "L" and (has_pv if i < NQ * NT else has_scores):
                            lo(i)
                        if kind == "M" and has_scores:
                            maximum_1(Home(uses, b, i, first_run), i)
                        if kind == "A" and has_pv:
                            add_sum(int(what[1]))
                            if not has_scores and int(what[1]) > 0:
                                final_sum(b, int(what[1]) - 1)
                            if not has_scores and int(what[1]) == NQ - 2:
                                offset_moment(b + 1, slot[U_STATS % 2])
                        if kind == "T" and has_scores:
                            theta_lo()
                        if kind == "G" and has_scores:
                            g_rows()
                        if has_scores and kind in "DRW":
                            {"D": offsets, "R": row_sums, "W": weights_1}[kind](int(what[1]))
                    if not has_scores and q == NQ - 2:
                        for c in range(NG):
                            chunk_stats(b + 1, c)
                        channel_stats(b + 1)

            def chunk_stats(b, c):
                if c % 2 == 0:
                    dve.wait_ge(s_x[c // 2], b * 16 + 16)
                dve.bn_stats(bst[:, c, :], xc[:, c * N:(c + 1) * N]).then_inc(s_bs, 1)

            def channel_stats(b):
                dve.wait_ge(s_bs, b * NG + NG)
                dve.memset(gn[:, 6:7], 0.0)
                dve.bn_aggr(mv[:, :], bst[:, :, :]).then_inc(s_mv, 1)

            def offset_moment(b, bank):
                dve.wait_ge(s_gm, b + 1)
                dve.wait_ge(s_mv, b + 1)
                dve.tensor_tensor(dmean, mv[:, 0:1], bank[:, 0:1], ALU.subtract).then_inc(s_dm, 1)
                dve.wait_ge(s_dm, b + 1)
                dve.scalar_tensor_tensor(out=e2, in0=dmean, scalar=dmean, in1=mv[:, 1:2], op0=ALU.mult,
                                         op1=ALU.add).then_inc(s_e2, 1)

            def gains(b, bank, done):
                dve.wait_ge(s_std, b + 1)
                dve.reciprocal(rstd, std).then_inc(s_rstd, 1)
                dve.tensor_copy(gmean, bank[:, 0:1]).then_inc(done, 1)
                dve.wait_ge(s_rstd, b + 1)
                dve.tensor_tensor(gain, rstd, gamma, ALU.mult).then_inc(s_gain, 1)

            def normalise(b, c):
                dve.wait_ge(s_gain, b + 1)
                cols = xc[:, c * QW:(c + 1) * QW]
                dve.tensor_scalar(cols, cols, gmean, gain, ALU.subtract, ALU.mult).then_inc(s_xn, 1)

            def final_sum(b, c):
                uses = Uses(dve, b)
                u = out_use(c)
                wait_full(dve, uses, u)
                cols = xr[:, c * QW:(c + 1) * QW]
                dve.scalar_tensor_tensor(out=cols, in0=slot[u % 2][:, :], scalar=bout, in1=cols,
                                         op0=ALU.add, op1=ALU.add).then_inc(s_free[u % 2], 1)

            dve.wait_ge(s_setup, 2)
            for c in range(NG):
                chunk_stats(0, c)
            channel_stats(0)
            offset_moment(0, pair[0])
            gains(0, pair[0], s_gmc)
            dve.wait_ge(s_gmc, 1)
            for c in range(NQ):
                normalise(0, c)
            with dve.Fori(0, B) as b:
                uses = Uses(dve, b)
                def low(u, j, src, dst, bias):
                    dve.wait_ge(s_ph, b * (2 * NQ) + j + 1)
                    minus(dst, slot[u % 2][:, :], bias, src).then_inc(s_free[u % 2], 1)

                for c in range(NQ):
                    low(U_PROJ + c, c, kh[:, c * QW:(c + 1) * QW], kl[:, c * QW:(c + 1) * QW], kb)
                low(U_PROJ + NQ, NQ, vh[:, 0:QW], vl[:, 0:QW], zero)
                dve.wait_ge(s_qhi, b * NG + 1)
                minus(ql, slot[U_Q0 % 2][:, 0:N], qb, qh).then_inc(s_free[U_Q0 % 2], 1)
                for t in range(NT):
                    wait_full(dve, uses, U_S0 + t)
                    dve.tensor_reduce(nm_first[:, t:t + 1], slot[(U_S0 + t) % 2][:, :], AXX, ALU.max,
                                      negate=True).then_inc(s_max, 1)
                for c in range(1, NQ):
                    low(U_V + c - 1, NQ + c, vh[:, c * QW:(c + 1) * QW], vl[:, c * QW:(c + 1) * QW], zero)
                with dve.Fori(0, NG - 1) as g:
                    group_0(b, g, False)
                group_0(b, NG - 1, True)

                phi_lo(b, 1)
                phi_lo(b, 2)
                dve.wait_ge(s_az, b + 1)
                iteration_1(b, -1, False, True)
                with dve.Fori(0, NG - 1) as g:
                    iteration_1(b, g, True, True)
                iteration_1(b, NG - 1, True, False)
                gains(b + 1, slot[U_STATS % 2], s_free[U_STATS % 2])
                wait_given_up(dve, uses, U_STATS)
                normalise(b + 1, 0)
                normalise(b + 1, 1)
                final_sum(b, NQ - 1)
                normalise(b + 1, 2)
                normalise(b + 1, 3)

        @block.gpsimd
        def _(pool):
            pool.memset(ident[:, :], 0.0).then_inc(s_const, 1)
            pool.memset(gmat[:, :], 1.0 / GROUP_CHANNELS)
            pool.memset(ones[:, :], 1.0)
            pool.memset(zeros[:, :], 0.0)
            for i in range(2):
                pool.memset(gwh[i][:, :, :], 0.0)
            blocks = gmat[:, :].rearrange("p (a c) -> p a c", c=GROUP_CHANNELS)
            pool.drain().then_inc(s_const, 1)
            pool.wait_ge(s_const, 3)
            pool.affine_select(out=ident[:, :], in_=ident[:, :], compare_op=ALU.not_equal, fill=1.0, base=0,
                               pattern=[[-1, P]], channel_multiplier=1)
            pool.affine_select(out=blocks, in_=blocks, compare_op=ALU.is_ge, fill=0.0, base=0,
                               pattern=[[-GROUP_CHANNELS, P // GROUP_CHANNELS], [0, GROUP_CHANNELS]],
                               channel_multiplier=1).then_inc(s_masks, 1)
            pool.wait_ge(s_masks, 1)
            pool.affine_select(out=blocks, in_=blocks, compare_op=ALU.is_ge, fill=0.0, base=GROUP_CHANNELS - 1,
                               pattern=[[GROUP_CHANNELS, P // GROUP_CHANNELS], [0, GROUP_CHANNELS]],
                               channel_multiplier=-1).then_inc(s_const, 1)

            def group_0(b, g, last):
                uses = Uses(pool, b, g, PER_G0)
                gi = Groups(pool, b, g, NG)
                for j in range(3):
                    wait_given_up(pool, uses, U_G0 + w_use(j, last))
                for i in range(2):
                    pool.wait_ge(s_oev[i], gi(2, CREDIT + 2))
                pool.tensor_tensor(osb, osb, wb, ALU.mult).then_inc(s_pr, 1)
                pool.wait_ge(s_pr, gi(1, CREDIT + 1))
                pool.tensor_tensor(wb[:, 0:QW], osb[:, 0:QW], osb[:, QW:2 * QW], ALU.add).then_inc(s_h1, 1)
                pool.wait_ge(s_h1, gi(1, CREDIT + 1))
                pool.tensor_tensor(xs[:, :], wb[:, 0:N], wb[:, N:2 * N], ALU.add).then_inc(s_h2, 1)
                pool.wait_ge(s_xb, b + 1)
                pool.wait_ge(s_h2, gi(1, CREDIT + 1))
                cols = xr[:, bass.ts(g, N)] if not last else xr[:, g * N:(g + 1) * N]
                pool.tensor_tensor(cols, cols, xs[:, :], ALU.add).then_inc(s_x1, 1)

            def iteration_1(b, g, has_pv, has_scores):
                first_run = not has_pv
                uses = Uses(pool, b, g, PER_G1)
                gi = Groups(pool, b, g, NG)
                rows = gsb[:, :].rearrange("p (t c) -> p t c", t=NT)
                part = gtmp[:, :].rearrange("p (t c) -> p t c", t=NS)
                for q in range(NQ):
                    if has_pv:
                        pool.wait_ge(s_acc[q % 2], gi(2, CREDIT + q // 2))
                        for t in range(NT):
                            if q == 0 and t in (HALVES[0].start, HALVES[1].start):
                                pool.wait_ge(s_w1[t // HALVES[1].start], gi(1, 1))
                            g_rows, weight = rows[:, t, :], wgt1[:, q, t:t + 1].broadcast_to([P, CI])
                            if t in WHOLE:
                                pool.tensor_tensor(gwh[q % 2][:, WHOLE.index(t), 0:CI], g_rows, weight,
                                                   ALU.mult).then_inc(s_gw, 1)
                                continue
                            i = SPLIT.index(t)
                            m = q * NS + i
                            hi_half, both = ghl[q % 2][:, i, 0:CI], part[:, i, :]
                            pool.tensor_tensor(both, g_rows, weight, ALU.mult).then_inc(s_gt, 1)
                            pool.wait_ge(s_gt, gi(NQ * NS, m + 1))
                            pool_copy(hi_half, both, zeros[:, 0:CI]).then_inc(s_gh, 1)
                            pool.wait_ge(s_gh, gi(NQ * NS, m + 1))
                            pool.tensor_tensor(ghl[q % 2][:, i, CI:P], both, hi_half.bitcast(F32),
                                               ALU.subtract).then_inc(s_g, 1)
                        pool.wait_ge(s_g, gi(NQ * NS, q * NS + NS))
                    if has_scores and q == 1:
                        if has_pv:
                            wait_given_up(pool, uses, use_1("g", False) - PER_G1)
                        else:
                            pool.wait_ge(s_x1, b * NG + NG)
                        pool_copy(xs[:, :], xr[:, bass.ds(g * N + N, N)], zeros[:, :]).then_inc(s_xs, 1)
                    if has_scores and q == NQ - 1:
                        wait_given_up(pool, uses, use_1("theta", first_run))
                        for t in range(NT):
                            home = Home(uses, b, q * NT + t, first_run)
                            pool.wait_ge(home.s_full, home.filled)
                            pool_copy(th[:, t * P:(t + 1) * P], tn[:, t * P:(t + 1) * P].bitcast(F32),
                                      zeros[:, 0:P]).then_inc(s_th, 1)

            pool.wait_ge(s_setup, 2)
            with pool.Fori(0, B) as b:
                pool.wait_ge(s_xr, b * 16 + 16)
                pool.tensor_tensor(xr[:, 0:L], xr[:, 0:L], vb.broadcast_to([P, L]), ALU.add).then_inc(s_xb, 1)
                with pool.Fori(0, NG - 1) as g:
                    group_0(b, g, False)
                zeros8 = zeros[:, :].unsqueeze(1).broadcast_to([P, NG, N])
                pool_copy(acc[:, :].rearrange("p (a n) -> p a n", a=NG), zeros8, zeros8).then_inc(s_az, 1)
                group_0(b, NG - 1, True)
                iteration_1(b, -1, False, True)
                with pool.Fori(0, NG - 1) as g:
                    iteration_1(b, g, True, True)
                iteration_1(b, NG - 1, True, False)


def kernel(**inputs):
    import numpy as np
    import concourse.bacc as bacc
    from concourse.bass_utils import run_bass_kernel_spmd as run

    nc = bacc.Bacc("TRN2", target_bir_lowering=False, num_devices=1)
    arrays = {}

    def given(name, a):
        a = np.ascontiguousarray(a)
        arrays[name] = a
        return nc.dram_tensor(name, a.shape, F32, kind="ExternalInput").ap()

    def col(a):
        return np.asarray(a).reshape(-1, 1)

    x = given("in_x", np.asarray(inputs["x"]).reshape(B, P, L))
    i0 = {k[len("L0_conv_"):]: np.asarray(v) for k, v in inputs.items() if k.startswith("L0_conv_")}
    i1 = {k[len("L1_conv_"):]: np.asarray(v) for k, v in inputs.items() if k.startswith("L1_conv_")}
    wth, bth = given("theta_w_t", i1["theta_w"].T), given("theta_b", col(i1["theta_b"]))
    wph, bph = given("phi_w_t", i1["phi_w"].T), given("phi_b", col(i1["phi_b"]))
    wout = given("W_w_t", i1["W_w"].T)
    w = [
        ("wq", given("wq_t", i0["wq"].T)), ("wk", given("wk_t", i0["wk"].T)), ("wv", given("wv", i0["wv"])),
        ("wo", given("wo_t", i0["wo"].T)), ("wg", given("g_w_t", i1["g_w"].T)),
        ("gbrow", given("g_b", i1["g_b"].reshape(1, -1))),
        ("gamma", given("gamma", col(i0["gamma"]))), ("beta", given("beta", col(i0["beta"]))),
        ("bq", given("bq", col(i0["bq"]))), ("bk", given("bk", col(i0["bk"]))),
        ("bv", given("bv", col(i0["bv"]))), ("bo", given("bo", col(i0["bo"]))),
        ("bout", given("W_b", col(i1["W_b"]))),
        ("wth0", wth), ("wth1", wth), ("wph0", wph), ("wph1", wph), ("wout0", wout), ("wout1", wout),
        ("bth0", bth), ("bth1", bth), ("bph0", bph), ("bph1", bph),
    ]
    out = nc.dram_tensor("out_0", (B, P, 64, 64), F32, kind="ExternalOutput").ap()
    build(nc, x, out.rearrange("b c h w -> b c (h w)"), w)
    r = run(nc, [arrays], core_ids=[0])
    return r.results[0]["out_0"]
```

```python
from contextlib import ExitStack

import concourse.bass as bass
from concourse import mybir

F32 = mybir.dt.float32
F32R = mybir.dt.float32r
ACT = mybir.ActivationFunctionType
ALU = mybir.AluOpType
AXX = mybir.AxisListType.X

P = 128
B = 4
L = 4096
CI = 64
N = 512
QW = 1024
NQ = L // QW
NT = N // P
NG = L // N
MT = QW // P
NM = NQ * MT
SCALE = float(P) ** -0.5
EPS = 1e-6
GROUP_CHANNELS = 4

SCORES_AT = [{0: 0, 1: 1, 3: 2, 4: 3}] * (NQ - 1) + [{0: 0, 1: 1, 4: 2, 5: 3}]
EXP_AT = [{1: 0, 2: 1, 4: 2, 5: 3}] * (NQ - 1) + [{1: 0, 2: 1, 5: 2, 6: 3}]
FIRST_1 = {(2, 6): "phi", (2, 7): "theta", (3, 1): 0, (3, 2): 1, (3, 4): 2, (3, 5): 3}
FIRST_EXP_1 = {(3, 2): 0, (3, 3): 1, (3, 5): 2, (3, 6): 3}
W_STEP = NM - MT + 4
PT_RING = 4
PV_LAG = 2
WHOLE = (0, 1)
SPLIT = (2, 3)
HALVES = (slice(0, 2), slice(2, 4))
NW, NS = len(WHOLE), len(SPLIT)
HL_RING = 4
PE_ORDER = ("SPSPPSSP", "PTSPSPPSS", "PSPSPSPS", "PGSPSSPSP")
ACT_ORDER = ("H2 H3 E0 E1 H6 E2 E3".split(), "H3 T0 E0 E1 H6 E2 E3".split(), "H3 E0 E1 H6 E2 E3".split(),
             "H3 E0 E1 D0 E2 E3 D1".split())
DVE_ORDER = ("M0 L2 M1 L3 M2 M3".split(), "L2 T0 M0 L3 M1 A0 M2 M3".split(), "L2 M0 L3 M1 A1 M2 M3".split(),
             "L2 G0 M0 L3 M1 D0 M2 A2 R0 M3 W0 D1 A3 R1 W1".split())

PROLOGUE = (("k", 0, None), ("q", 0, 0), ("k", 1, None), ("k", 2, 1), ("s", 0, None), ("k", 3, 0), ("s", 1, None),
            ("v", 0, None), ("s", 2, None), ("v", 1, 1), ("s", 3, None), ("v", 2, None), ("v", 3, None))
ACT_PROLOGUE = [PROLOGUE[i] for i in (0, 1, 2, 3, 5, 4, 7, 6, 9, 8, 10, 11, 12)]
IN_SLOT = [(what, i) for what, i, place in PROLOGUE if place is None]
IN_PAIR = [[(what, i) for what, i, place in PROLOGUE if place == p] for p in range(2)]
U_S0 = IN_SLOT.index(("s", 0))
U_G0 = len(IN_SLOT)
PER_G0 = NQ * NT + 1 + 3
U_PHI0 = U_G0 + PER_G0 * (NG - 1) + (NQ - 1) * NT
U_TH0 = U_PHI0 + 1
U_FIRST = U_TH0 + 1
U_PHI1 = U_FIRST + NT + 3
U_BEGIN = U_PHI1 + 2
BEGIN = ("theta", 4, 6, "phi", 8, 10, "g", 12, 14)
PER_G1 = NQ * NT + 2
U_G1 = U_BEGIN + len(BEGIN) - PER_G1
PAIR_USES = len(IN_PAIR[0]) + (NQ - 1) * NT // 4
assert len(IN_PAIR[0]) == len(IN_PAIR[1])
U_OUT = U_G1 + PER_G1 * NG
U_STATS = U_OUT + 2
USES = U_OUT + NQ + 1
WROW = 32
CREDIT = 1
assert USES % 2 == 0 and PER_G0 % 2 == 0 and PER_G1 % 2 == 0


def score_use_0(q, t):
    return q * NT + t + (1 + (t >= 2) if q == NQ - 1 else 0)


PREV_S = U_G0 + score_use_0(NQ - 1, 0) - PER_G0
PREV_LAST = [U_G0 + score_use_0(NQ - 1, t) - PER_G0 for t in (2, 3)]
assert PREV_S == U_S0 and PREV_LAST == [IN_SLOT.index(("s", t)) for t in (2, 3)]
U_QPROJ = (NQ - 1) * NT


def w_use(j, last):
    first = U_FIRST - U_G0 - PER_G0 * (NG - 1) if last else score_use_0(NQ - 1, 0)
    return first + (2 if j == 0 else NT + j)


def phi_use(c):
    return {0: U_PHI0, NQ - 1: U_BEGIN + BEGIN.index("phi")}.get(c, U_PHI1 + c - 1)


def out_use(c):
    return U_OUT + c + (U_OUT + c >= U_STATS)


U_TH, U_G = NT, (NQ - 1) * NT + 1


def use_1(what, first):
    return PER_G1 + (U_BEGIN + BEGIN.index(what) if first else U_G1 + {"theta": U_TH, "g": U_G}[what])


def score_use_1(n, first):
    if first:
        return PER_G1 + (U_FIRST + n + (n >= 2) if n < NT else U_BEGIN + BEGIN.index(n))
    return PER_G1 + U_G1 + n + (n >= NT) + (n >= (NQ - 1) * NT)


def build(nc, x, out, w):
    with ExitStack() as ctx:
        def sb(name, shape, dt=F32):
            return ctx.enter_context(nc.sbuf_tensor(name, shape, dt))

        def sem(name):
            return ctx.enter_context(nc.semaphore(name))

        slot = [ctx.enter_context(nc.psum_tensor(f"score_slot{i}", [P, QW], F32)) for i in range(2)]
        pair = [ctx.enter_context(nc.psum_tensor(f"bank_pair{i}", [P, QW], F32)) for i in range(2)]
        t_bank = [pair[0][:, i * N:(i + 1) * N] for i in range(2)]
        o_bank = [pair[1][:, i * N:(i + 1) * N] for i in range(2)]

        r = sb("operands_r", [P, 4 * L + 2 * N + PT_RING * 2 * N], F32R)
        kh, kl = r[:, 0:L], r[:, L:2 * L]
        vh, vl = r[:, 2 * L:3 * L], r[:, 3 * L:4 * L]
        o = 4 * L
        qh, ql = r[:, o:o + N], r[:, o + N:o + 2 * N]
        th, tn = qh, ql
        o += 2 * N
        pth = [r[:, o + i * 2 * N:o + i * 2 * N + N] for i in range(PT_RING)]
        ptl = [r[:, o + i * 2 * N + N:o + (i + 1) * 2 * N] for i in range(PT_RING)]
        phh, phl = kh, kl
        hlh = [r[:, 2 * L + i * 2 * QW:2 * L + i * 2 * QW + QW] for i in range(HL_RING)]
        hll = [r[:, 2 * L + i * 2 * QW + QW:2 * L + (i + 1) * 2 * QW] for i in range(HL_RING)]
        ghl = [r[:, o + i * N:o + (i + 1) * N].rearrange("p (t c) -> p t c", t=NT) for i in range(2)]

        f = sb("work", [P, NQ, NT, QW])
        xc = f[:, 0, :, :].rearrange("p t n -> p (t n)")
        p0 = [f[:, 1 + i, :, :] for i in range(2)]
        osb = f[:, 3, 0:2, :].rearrange("p t n -> p (t n)")
        wb = f[:, 3, 2:4, :].rearrange("p t n -> p (t n)")
        xr = sb("x_residual", [P, L + N])
        acc = sb("acc", [P, L])
        xs = sb("x_stage", [P, N])
        zeros = sb("zeros", [P, N])
        gsb = sb("g_rows", [P, NT * CI])
        gtmp = sb("g_weighted", [P, NS * CI])
        gwh = [sb(f"g_whole{i}", [P, NW, P]) for i in range(2)]

        ident, gmat, ones = sb("ident", [P, P]), sb("gmat", [P, P]), sb("ones", [P, P])
        pick_both, pick_tile = sb("pick", [P, NQ * NT]), sb("pick_tile", [P, NT])
        pick_q, pick_quarter = sb("pick_q", [P, NQ]), sb("pick_quarter", [P, NQ], F32R)
        wq, wqs, wk, wv, wo, wvo = [sb(n + "_sb", [P, P]) for n in ("wq", "wqs", "wk", "wv", "wo", "wvo")]
        wth, wph, wout = [sb(n, [P, P]) for n in ("wth_sb", "wph_sb", "wout_sb")]
        wg = sb("wg_sb", [P, CI])
        vec = sb("vec", [P, 16])
        gamma, beta, bq, bk, bv, bo, bth, bph, bout = [vec[:, i:i + 1] for i in range(9)]
        qb, kb, vb, zero, eps = [vec[:, i:i + 1] for i in range(9, 14)]
        gbrow, gbb = sb("gbrow_sb", [1, CI]), sb("gbb", [P, CI])

        bst, mv = sb("bst", [P, NG, 6]), sb("mv", [P, 2])
        gn = sb("gn", [P, 8])
        dmean, e2, std, rstd, gmean, gain = [gn[:, i:i + 1] for i in range(6)]
        st0 = sb("st0", [P, 8 * 16])
        nm_first, z_first = st0[:, 0:NT], st0[:, NT:2 * NT]
        nmg = st0[:, 16:32].rearrange("p (q t) -> p q t", q=NQ)
        zg = st0[:, 32:48].rearrange("p (q t) -> p q t", q=NQ)
        nmin, zsum, zrec = st0[:, 8:12], st0[:, 12:16], st0[:, 48:52]
        diff, efac = st0[:, 64:80], st0[:, 80:96]
        ez = st0[:, 96:112]
        w2 = sb("weights_twice", [P, P])
        wt2 = sb("weights_transposed", [2 * WROW, P], F32R)
        wspread = sb("weights_spread", [2 * WROW, N], F32R)
        st1 = sb("st1", [P, 8 * 16])
        nm1 = st1[:, 0:16].rearrange("p (q t) -> p q t", q=NQ)
        z1 = st1[:, 16:32].rearrange("p (q t) -> p q t", q=NQ)
        nmin1, zsum1, zrec1 = st1[:, 32:36], st1[:, 36:40], st1[:, 40:44]
        diff1, efac1, ez1, wgt1 = [st1[:, 48 + 16 * i:64 + 16 * i].rearrange("p (q t) -> p q t", q=NQ)
                                   for i in range(4)]

        def qt(a):
            return a.rearrange("p (q t) -> p q t", q=NQ)

        def tq(a):
            return a.rearrange("p q t -> p t q")

        s_wl = sem("weights_loaded")
        s_const, s_setup_pe, s_setup = sem("constants"), sem("setup_products"), sem("setup_done")
        s_full = [sem(f"slot_full{i}") for i in range(2)]
        s_free = [sem(f"slot_free{i}") for i in range(2)]
        s_pair_full = [sem(f"pair_full{i}") for i in range(2)]
        s_pair_free = [sem(f"pair_free{i}") for i in range(2)]
        s_x = [sem(f"x_loaded{i}") for i in range(NQ)]
        s_bs, s_mv, s_gm, s_dm, s_e2, s_std, s_rstd, s_gain = [
            sem(n) for n in ("chunk_stats", "channel_stats", "group_mean", "mean_offset", "second_moment",
                             "std", "rstd", "gain")]
        s_xr, s_xb, s_xn = sem("residual_loaded"), sem("residual_biased"), sem("x_normalised")
        s_gm2, s_gmc = sem("group_second_moment"), sem("group_mean_copied")
        s_ph = sem("projection_hi")
        s_qhi = sem("q_hi")
        s_max, s_cp = sem("max0"), sem("first_quarter_stats")
        s_t = [sem(f"transposed{i}") for i in range(2)]
        s_hi = sem("pt_hi")
        s_lo = [sem(f"pt_lo{i}") for i in range(2)]
        s_pv = [sem(f"pv_done{i}") for i in range(PT_RING)]
        s_oev = [sem(f"sum_evacuated{i}") for i in range(2)]
        s_mn, s_df, s_e, s_ez, s_zs, s_zr, s_w, s_wh, s_wx = [
            sem(n) for n in ("nmin0", "diff0", "efac0", "ez0", "zsum0", "zrec0", "wgt0", "w_hi0", "w_spread0")]
        s_pr, s_h1, s_h2, s_x1 = sem("weighted"), sem("half_sum"), sem("quarter_sum"), sem("x1_group")
        s_phi = sem("phi_hi")
        s_thh, s_th, s_xs = sem("theta_hi"), sem("theta_staged"), sem("x_staged")
        s_az = sem("acc_zeroed")
        s_max1, s_hi1, s_lo1 = sem("max1"), sem("p1_hi"), sem("p1_lo")
        s_mn1, s_df1, s_e1, s_ez1, s_zs1, s_zr1, s_w1 = [
            [sem(f"{n}_{half}") for half in ("whole", "split")]
            for n in ("nmin1", "diff1", "efac1", "ez1", "zsum1", "zrec1", "wgt1")]
        s_gw, s_gt, s_gh, s_g = sem("g_whole_ready"), sem("g_weighted"), sem("g_hi"), sem("g_ready")
        s_masks, s_pick = sem("masks_ready"), sem("picks_ready")
        s_pvs = [sem(f"pv1_split{i}") for i in range(HL_RING)]
        s_pvf = sem("pv1_whole")
        s_acc = [sem(f"acc_added{i}") for i in range(2)]
        s_out = sem("stored")

        class Groups:

            def __init__(self, eng, b, g, groups):
                self.eng, self.made = eng, {}
                self.run, self.off = (b * groups, g) if isinstance(g, int) else (b * groups + g, 0)

            def __call__(self, k, n):
                if k not in self.made:
                    self.made[k] = self.eng.snap(self.run * k)
                return self.made[k] + (self.off * k + n)

        class Uses:

            def __init__(self, eng, b, g=0, per=0):
                fixed = isinstance(g, int)
                run = b * (USES // 2) if fixed else b * (USES // 2) + g * (per // 2)
                self.base = run if isinstance(run, int) else eng.snap(run)
                self.off = g * (per // 2) if fixed else 0

            def before(self, u):
                return self.base + (CREDIT + self.off + u // 2)

            def done(self, u):
                return self.base + (self.off + u // 2 + 1)

        class Home:

            def __init__(self, bank, full, filled, free, before, given_up):
                self.bank, self.s_full, self.filled = bank, full, filled
                self.s_free, self.before, self.given_up = free, before, given_up

        def slot_home(uses, u):
            before = uses.before(u)
            return Home(slot[u % 2], s_full[u % 2], uses.done(u), s_free[u % 2], before, before + 1)

        def pair_home(b, i, k):
            return Home(pair[i], s_pair_full[i], b * PAIR_USES + k + 1, s_pair_free[i],
                        b * PAIR_USES + k if k else None, b * PAIR_USES + k + 1)

        def score_home(uses, b, n, first):
            if first and n >= NT and n % 2:
                k, i = divmod((n - NT) // 2, 2)
                return pair_home(b, i, len(IN_PAIR[i]) + k)
            return slot_home(uses, score_use_1(n, first))

        def prologue_home(uses, b, what, i, place):
            if place is None:
                return slot_home(uses, IN_SLOT.index((what, i)))
            return pair_home(b, place, IN_PAIR[place].index((what, i)))

        def wait_full(eng, uses, u):
            eng.wait_ge(s_full[u % 2], uses.done(u))

        def wait_given_up(eng, uses, u):
            eng.wait_ge(s_free[u % 2], uses.before(u) + 1)

        def pool_copy(dst, src, n):
            return nc.gpsimd.tensor_tensor(dst, src, n, ALU.add)

        def load_weights(eng, some):
            for dst, src in some:
                tile = {"wq": wq, "wk": wk, "wv": wv, "wo": wo, "wg": wg, "gbrow": gbrow, "gamma": gamma,
                        "beta": beta, "bq": bq, "bk": bk, "bv": bv, "bo": bo, "bout": bout,
                        "wth0": wth[:, 0:CI], "wth1": wth[:, CI:P], "wph0": wph[:, 0:CI], "wph1": wph[:, CI:P],
                        "wout0": wout[0:CI, :], "wout1": wout[CI:P, :],
                        "bth0": vec[0:CI, 6:7], "bth1": vec[CI:P, 6:7],
                        "bph0": vec[0:CI, 7:8], "bph1": vec[CI:P, 7:8]}[dst]
                eng.dma_start(tile[:, :] if hasattr(tile, "name") else tile, src).then_inc(s_wl, 16)

        block = ctx.enter_context(nc.Block())

        @block.sync
        def _(sp):
            for s in (*s_free, *s_lo, *s_oev, *s_pv, *s_t, *s_pvs, *s_acc, s_pr, s_h1, s_h2):
                sp.sem_inc(s, CREDIT)
            sp.sem_inc(s_out, 16 * CREDIT)
            def load(b):
                for c in range(NQ):
                    sp.dma_start(xc[:, c * QW:(c + 1) * QW], x[b, :, c * QW:(c + 1) * QW]).then_inc(s_x[c], 16)

            def store(b):
                uses = Uses(sp, b)
                for c in range(NQ):
                    wait_given_up(sp, uses, out_use(c))
                    sp.dma_start(out[b, :, c * QW:(c + 1) * QW], xr[:, c * QW:(c + 1) * QW]).then_inc(s_out, 16)

            def load_residual(b):
                sp.dma_start(xr[:, 0:L], x[b, :, :]).then_inc(s_xr, 16)

            def end_of_batch(b, following):
                sp.wait_ge(s_pvs[NS - 1], b * (NG * NQ * NS // HL_RING) + (NG - 1) * (NQ * NS // HL_RING) + 1 + CREDIT)
                load(following)
                store(b)

            load(0)
            load_weights(sp, w[0::2])
            load_residual(0)
            with sp.Fori(0, B - 1) as b:
                end_of_batch(b, b + 1)
                sp.wait_ge(s_out, b * (16 * NQ) + 16 * (NQ + CREDIT))
                load_residual(b + 1)
            end_of_batch(B - 1, 0)
            sp.wait_ge(s_out, 16 * (NQ * B + CREDIT))

        @block.tensor
        def _(pe):
            mm = pe.matmul
            pe.wait_ge(s_wl, 16 * len(w))
            pe.wait_ge(s_const, 4)
            mm(pair[0][:, 0:P], wv[:, :], wo[:, :], start=True, stop=True)
            mm(pair[1][:, 0:1], wq[:, :], beta, start=True, stop=True)
            mm(pair[1][:, 1:2], wk[:, :], beta, start=True, stop=True)
            mm(pair[1][:, 2:2 + CI], ones[0:1, :], gbrow[:, :], start=True, stop=True).then_inc(s_setup_pe, 1)
            pe.wait_ge(s_setup, 1)
            mm(pair[0][:, N:N + 1], wvo[:, :], beta, start=True, stop=False)
            mm(pair[0][:, N:N + 1], wo[:, :], bv, start=False, stop=True).then_inc(s_setup_pe, 1)
            pe.wait_ge(s_setup, 2)

            def scores_0(home, q, t):
                pe.wait_ge(home.s_free, home.before)
                s = home.bank
                for a, kk, first, last in ((qh, kh, True, False), (qh, kl, False, False), (ql, kh, False, True)):
                    for c in range(2):
                        ins = mm(s[:, c * N:(c + 1) * N], a[:, t * P:(t + 1) * P],
                                 kk[:, q * QW + c * N:q * QW + (c + 1) * N], start=first, stop=last)
                ins.then_inc(home.s_full, 1)

            def qproj(home, cols):
                if home.before is not None:
                    pe.wait_ge(home.s_free, home.before)
                mm(home.bank[:, 0:N], wqs[:, :], cols, start=True, stop=True).then_inc(home.s_full, 1)

            def group_0(b, g, last):
                uses = Uses(pe, b, g, PER_G0)
                gi = Groups(pe, b, g, NG)

                def transpose(n):
                    if n % MT == 0:
                        for u in [U_G0 + score_use_0(n // MT - 1, t) for t in (2, 3)] if n else PREV_LAST:
                            wait_given_up(pe, uses, u)
                    pe.wait_ge(s_lo[n % 2], gi(NM // 2, CREDIT + n // 2))
                    for t in range(NT):
                        ins = pe.transpose(t_bank[n % 2][:, t * P:(t + 1) * P],
                                           p0[(n // MT) % 2][:, t, (n % MT) * P:(n % MT + 1) * P], ident[:, :])
                    ins.then_inc(s_t[n % 2], 1)

                def pv(n):
                    q, j = n // MT, n % MT
                    if j == 0:
                        pe.wait_ge(s_oev[q % 2], gi(2, CREDIT + q // 2))
                    pe.wait_ge(s_lo[n % 2], gi(NM // 2, CREDIT + n // 2 + 1))
                    ob, c = o_bank[q % 2], slice(n * P, (n + 1) * P)
                    mm(ob, vh[:, c], pth[n % PT_RING], start=(j == 0), stop=False)
                    mm(ob, vl[:, c], pth[n % PT_RING], start=False, stop=False)
                    mm(ob, vh[:, c], ptl[n % PT_RING], start=False, stop=(j == MT - 1)).then_inc(
                        s_pv[n % PT_RING], 1)

                def weights_transpose():
                    u = U_G0 + w_use(0, last)
                    pe.wait_ge(s_w, gi(1, 1))
                    pe.wait_ge(s_free[u % 2], uses.before(u))
                    pe.transpose(slot[u % 2][:, 0:P], w2[:, :], ident[:, :]).then_inc(s_full[u % 2], 1)

                def weights(j):
                    u = U_G0 + w_use(j, last)
                    pe.wait_ge(s_wx, gi(1, 1))
                    pe.wait_ge(s_free[u % 2], uses.before(u))
                    for i in range(2):
                        q = 2 * j - 2 + i
                        ins = mm(slot[u % 2][:, i * N:(i + 1) * N],
                                 pick_quarter[0:2 * WROW, q:q + 1].broadcast_to([2 * WROW, P]), wspread[:, :],
                                 start=True, stop=True)
                    ins.then_inc(s_full[u % 2], 1)

                for n in range(NM):
                    q, j = n // MT, n % MT
                    transpose(n)
                    if n == W_STEP:
                        pv(n - PV_LAG)
                        weights_transpose()
                    if j in SCORES_AT[q] and not (last and q == NQ - 1):
                        t = SCORES_AT[q][j]
                        if q == NQ - 1 and t == 0:
                            wait_given_up(pe, uses, U_G0 + U_QPROJ)
                        scores_0(slot_home(uses, U_G0 + score_use_0(q, t)), (q + 1) % NQ, t)
                    if q == NQ - 2 and j == 6 and not last:
                        qproj(slot_home(uses, U_G0 + U_QPROJ), xc[:, bass.ts(g + 1, N)])
                    if last and (q, j) in FIRST_1:
                        t = FIRST_1[q, j]
                        if t == "phi":
                            phi(b, 0)
                        elif t == "theta":
                            theta_first(b)
                        else:
                            if t == 0:
                                wait_given_up(pe, Uses(pe, b), U_PHI0)
                                wait_given_up(pe, Uses(pe, b), U_TH0)
                            scores_1(score_home(Uses(pe, b, -1, PER_G1), b, t, True), t)
                    if q == NQ - 1 and j == 7:
                        weights(1)
                    if n >= PV_LAG and n != W_STEP:
                        pv(n - PV_LAG)
                pv(NM - 2)
                weights(2)
                pv(NM - 1)

            def scores_1(home, n):
                q, t = n // NT, n % NT
                if home.before is not None:
                    pe.wait_ge(home.s_free, home.before)
                for ph, first in ((phh, True), (phl, False)):
                    for c in range(2):
                        ins = mm(home.bank[:, c * N:(c + 1) * N], th[:, t * P:(t + 1) * P],
                                 ph[:, q * QW + c * N:q * QW + (c + 1) * N], start=first, stop=not first)
                ins.then_inc(home.s_full, 1)

            def phi(b, c):
                uses, u = Uses(pe, b), phi_use(c)
                pe.wait_ge(s_x1, b * NG + (c + 1) * (QW // N))
                pe.wait_ge(s_free[u % 2], uses.before(u))
                for i in range(2):
                    ins = mm(slot[u % 2][:, i * N:(i + 1) * N], wph[:, :],
                             xr[:, c * QW + i * N:c * QW + (i + 1) * N], start=True, stop=True)
                ins.then_inc(s_full[u % 2], 1)

            def theta_first(b):
                uses = Uses(pe, b)
                pe.wait_ge(s_free[U_TH0 % 2], uses.before(U_TH0))
                mm(slot[U_TH0 % 2][:, 0:N], wth[:, :], xr[:, 0:N], start=True, stop=True).then_inc(
                    s_full[U_TH0 % 2], 1)

            def iteration_1(b, g, has_pv, has_scores):
                first_run = not has_pv
                uses = Uses(pe, b, g, PER_G1)
                gi = Groups(pe, b, g, NG)

                def scores(n):
                    if n < NT:
                        pe.wait_ge(s_th, gi(NT, n + 1))
                    home = score_home(uses, b, n, first_run)
                    if first_run and n in (NT + 1, NT + 3):
                        for i in range(2):
                            pe.wait_ge(s_oev[i], b * (2 * NG) + 2 * NG + CREDIT)
                    scores_1(home, n)

                def theta():
                    u = use_1("theta", first_run)
                    pe.wait_ge(s_free[u % 2], uses.before(u))
                    mm(slot[u % 2][:, 0:N], wth[:, :], xr[:, bass.ds(g * N + 2 * N, N)],
                       start=True, stop=True).then_inc(s_full[u % 2], 1)

                def grows():
                    u = use_1("g", first_run)
                    pe.wait_ge(s_xs, gi(1, 2))
                    pe.wait_ge(s_free[u % 2], uses.before(u))
                    for t in range(NT):
                        ins = mm(slot[u % 2][:, t * CI:(t + 1) * CI], xs[:, t * P:(t + 1) * P], wg[:, :],
                                 start=True, stop=True)
                    ins.then_inc(s_full[u % 2], 1)

                def pv(n):
                    q, t = n // NT, n % NT
                    a = pair[q % 2]
                    if t == 0:
                        pe.wait_ge(s_acc[q % 2], gi(2, CREDIT + q // 2))
                    if t in WHOLE:
                        i = WHOLE.index(t)
                        pe.wait_ge(s_gw, gi(NQ * NW, q * NW + i + 1))
                        for c in range(2):
                            ins = mm(a[:, c * N:(c + 1) * N], gwh[q % 2][:, i, :],
                                     f[:, q, t, c * N:(c + 1) * N], start=(t == 0), stop=False)
                        ins.then_inc(s_pvf, 1)
                    else:
                        i = SPLIT.index(t)
                        m = q * NS + i
                        pe.wait_ge(s_g, gi(NQ * NS, m + 1))
                        pe.wait_ge(s_lo1, gi(NQ * NS, m + 1))
                        for part in (hlh, hll):
                            for c in range(2):
                                ins = mm(a[:, c * N:(c + 1) * N], ghl[q % 2][:, i, :],
                                         part[m % HL_RING][:, c * N:(c + 1) * N],
                                         start=False, stop=(t == NT - 1 and part is hll))
                        ins.then_inc(s_pvs[m % HL_RING], 1)

                for q in range(1 if first_run else 0, NQ):
                    if first_run and q == NQ - 2:
                        phi(b, NQ - 1)
                    ns = np_ = 0
                    for what in PE_ORDER[q]:
                        if what == "P" and has_pv:
                            pv(q * NT + np_)
                            np_ += 1
                        if what == "T" and has_scores:
                            theta()
                        if what == "G" and has_scores:
                            grows()
                        if what == "S" and has_scores:
                            scores(q * NT + ns)
                            ns += 1
                        if not has_scores and q == NQ - 1 and what == "P" and np_ == 2:
                            group_mean(b + 1, slot[U_STATS % 2], Uses(pe, b))
                    if not has_scores and q == NQ - 1:
                        group_second_moment(b + 1, slot[U_STATS % 2], s_full[U_STATS % 2])
                    if not has_scores and q > 0:
                        project_out(b, q - 1)

            def project_out(b, c):
                uses = Uses(pe, b)
                u = out_use(c)
                pe.wait_ge(s_acc[c % 2], b * (NG * 2) + (NG - 1) * 2 + c // 2 + 1 + CREDIT)
                pe.wait_ge(s_free[u % 2], uses.before(u))
                for i in range(2):
                    ins = mm(slot[u % 2][:, i * N:(i + 1) * N], wout[:, :],
                             acc[:, c * QW + i * N:c * QW + (i + 1) * N], start=True, stop=True)
                ins.then_inc(s_full[u % 2], 1)

            def group_mean(b, bank, uses):
                pe.wait_ge(s_mv, b + 1)
                if uses:
                    pe.wait_ge(s_free[U_STATS % 2], uses.before(U_STATS))
                mm(bank[:, 0:1], gmat[:, :], mv[:, 0:1], start=True, stop=True).then_inc(s_gm, 1)

            def group_second_moment(b, bank, done):
                pe.wait_ge(s_e2, b + 1)
                mm(bank[:, N:N + 1], gmat[:, :], e2, start=True, stop=True).then_inc(done, 1)

            group_mean(0, pair[0], None)
            group_second_moment(0, pair[0], s_gm2)
            with pe.Fori(0, B) as b:
                uses = Uses(pe, b)

                def project(home, c, is_k):
                    pe.wait_ge(s_xn, b * NQ + c + 1)
                    if home.before is not None:
                        pe.wait_ge(home.s_free, home.before)
                    if is_k:
                        for i in range(2):
                            ins = mm(home.bank[:, i * N:(i + 1) * N], wk[:, :],
                                     xc[:, c * QW + i * N:c * QW + (i + 1) * N], start=True, stop=True)
                    else:
                        for i in range(MT):
                            ins = mm(home.bank[:, i * P:(i + 1) * P], xc[:, c * QW + i * P:c * QW + (i + 1) * P],
                                     wvo[:, :], start=True, stop=True)
                    ins.then_inc(home.s_full, 1)

                q_home = prologue_home(uses, b, "q", 0, 0)
                for what, i, place in PROLOGUE:
                    home = prologue_home(uses, b, what, i, place)
                    if what == "q":
                        qproj(home, xc[:, 0:N])
                    elif what == "s":
                        if i == 0:
                            pe.wait_ge(q_home.s_free, q_home.given_up)
                        scores_0(home, 0, i)
                    else:
                        project(home, i, what == "k")
                with pe.Fori(0, NG - 1) as g:
                    group_0(b, g, False)
                group_0(b, NG - 1, True)

                phi(b, 1)
                phi(b, 2)
                iteration_1(b, -1, False, True)
                with pe.Fori(0, NG - 1) as g:
                    iteration_1(b, g, True, True)
                iteration_1(b, NG - 1, True, False)
                project_out(b, NQ - 1)

        @block.scalar
        def _(act):
            load_weights(act, w[1::2])

            def exp0(home, t, nm, z, dst):
                act.activation(dst, home.bank[:, :], ACT.Exp, bias=nm, accum_out=z).then_inc(home.s_free, 1)

            def phi_hi(b, c):
                u = phi_use(c)
                wait_full(act, Uses(act, b), u)
                act.activation(phh[:, c * QW:(c + 1) * QW], slot[u % 2][:, :], ACT.Identity,
                               bias=bph).then_inc(s_phi, 1)

            def exp_1(home, n):
                q, t = n // NT, n % NT
                act.activation(f[:, q, t, :], home.bank[:, :], ACT.Exp, bias=nm1[:, q, t:t + 1],
                               accum_out=z1[:, q, t:t + 1]).then_inc(home.s_free, 1)

            def group_0(b, g, last):
                uses = Uses(act, b, g, PER_G0)
                gi = Groups(act, b, g, NG)

                def hi(n):
                    act.wait_ge(s_t[n % 2], gi(NM // 2, CREDIT + n // 2 + 1))
                    act.wait_ge(s_pv[n % PT_RING], gi(NM // PT_RING, CREDIT + n // PT_RING))
                    act.activation(pth[n % PT_RING], t_bank[n % 2], ACT.Copy).then_inc(s_hi, 1)

                def sum_out(q):
                    n = q * MT + MT - 1
                    act.wait_ge(s_h1, gi(1, CREDIT + 0))
                    act.wait_ge(s_pv[n % PT_RING], gi(NM // PT_RING, CREDIT + n // PT_RING + 1))
                    act.activation(osb[:, q * N:(q + 1) * N], o_bank[q % 2], ACT.Copy).then_inc(s_oev[q % 2], 1)

                def weights_out(j):
                    u = U_G0 + w_use(j, last)
                    wait_full(act, uses, u)
                    act.wait_ge(s_h2, gi(1, CREDIT + 0))
                    act.activation(wb[:, (j - 1) * QW:j * QW], slot[u % 2][:, :], ACT.Copy).then_inc(s_free[u % 2], 1)

                for n in range(NM):
                    q, j = n // MT, n % MT
                    hi(n)
                    if q == NQ - 2 and j == 6 and not last:
                        wait_full(act, uses, U_G0 + U_QPROJ)
                        act.activation(qh, slot[(U_G0 + U_QPROJ) % 2][:, 0:N], ACT.Identity, bias=qb).then_inc(
                            s_qhi, 1)
                    if q == NQ - 1 and j == 1:
                        act.wait_ge(s_df, gi(1, 1))
                        act.activation(efac, diff, ACT.Exp).then_inc(s_e, 1)
                    if n == W_STEP:
                        u = U_G0 + w_use(0, last)
                        wait_full(act, uses, u)
                        act.activation(wt2[:, :], slot[u % 2][0:2 * WROW, 0:P], ACT.Copy).then_inc(s_wh, 1)
                    if last and FIRST_1.get((q, j)) == "phi":
                        phi_hi(b, 0)
                    if last and FIRST_1.get((q, j)) == "theta":
                        wait_full(act, Uses(act, b), U_TH0)
                        act.activation(th, slot[U_TH0 % 2][:, 0:N], ACT.Identity, bias=bth).then_inc(s_thh, 1)
                    if last and (q, j) in FIRST_EXP_1:
                        t = FIRST_EXP_1[q, j]
                        act.wait_ge(s_max1, b * (NG * NQ * NT) + t + 1)
                        exp_1(score_home(Uses(act, b, -1, PER_G1), b, t, True), t)
                    if j in EXP_AT[q] and not (last and q == NQ - 1):
                        t = EXP_AT[q][j]
                        u = U_G0 + score_use_0(q, t)
                        act.wait_ge(s_max, gi(NQ * NT, NT * (q + 1) + t + 1))
                        if t == 0:
                            act.wait_ge(s_t[1], gi(NM // 2, CREDIT + q * (MT // 2)))
                        if q == NQ - 1:
                            exp0(slot_home(uses, u), t, nm_first[:, t:t + 1], z_first[:, t:t + 1], p0[0][:, t, :])
                        else:
                            exp0(slot_home(uses, u), t, nmg[:, q + 1, t:t + 1], zg[:, q + 1, t:t + 1],
                                 p0[(q + 1) % 2][:, t, :])
                    if j == PV_LAG + 1 and q > 0:
                        sum_out(q - 1)
                weights_out(1)
                weights_out(2)
                sum_out(NQ - 1)

            def iteration_1(b, g, has_pv, has_scores):
                first_run = not has_pv
                uses = Uses(act, b, g, PER_G1)
                gi = Groups(act, b, g, NG)

                def hi(n):
                    q, t = n // NT, n % NT
                    if q == NQ:
                        home = score_home(uses, b, t, first_run)
                        act.wait_ge(home.s_free, home.given_up)
                    m = q * NS + SPLIT.index(t)
                    act.wait_ge(s_pvs[m % HL_RING], gi(NQ * NS // HL_RING, CREDIT + m // HL_RING))
                    act.activation(hlh[m % HL_RING], f[:, q % NQ, t, :], ACT.Copy).then_inc(s_hi1, 1)

                def theta_hi():
                    u = use_1("theta", first_run)
                    wait_full(act, uses, u)
                    if has_pv:
                        act.wait_ge(s_th, gi(NT, NT))
                    act.activation(tn, slot[u % 2][:, 0:N], ACT.Identity, bias=bth).then_inc(s_thh, 1)

                def exp1(n):
                    q, t = n // NT, n % NT
                    act.wait_ge(s_max1, gi(NQ * NT, NQ * NT + n + 1))
                    if has_pv and t in WHOLE:
                        act.wait_ge(s_pvf, gi(NQ * NW, q * NW + WHOLE.index(t) + 1))
                    elif has_pv:
                        act.wait_ge(s_lo1, gi(NQ * NS, q * NS + SPLIT.index(t) + 1))
                    exp_1(score_home(uses, b, n, first_run), n)

                def efac(h):
                    act.wait_ge(s_df1[h], gi(1, 2))
                    act.activation(efac1[:, :, HALVES[h]], diff1[:, :, HALVES[h]], ACT.Exp).then_inc(s_e1[h], 1)

                for q in range(1 if first_run else 0, NQ):
                    if first_run and q == NQ - 2:
                        phi_hi(b, NQ - 1)
                    for what in ACT_ORDER[q]:
                        kind, i = what[0], int(what[1])
                        if kind == "H" and (has_pv if q * NT + i < NQ * NT else has_scores):
                            hi(q * NT + i)
                        if kind == "T" and has_scores:
                            theta_hi()
                        if kind == "E" and has_scores:
                            exp1(q * NT + i)
                        if kind == "D" and has_scores:
                            efac(i)

            def root(bank):
                act.activation(std, bank[:, N:N + 1], ACT.Sqrt, bias=eps).then_inc(s_std, 1)
                act.activation(gn[:, 7:8], zero, ACT.Exp)

            act.wait_ge(s_const, 4)
            act.activation(vec[:, 14:15], ones[:, 0:1], ACT.Sqrt)
            act.wait_ge(s_setup, 2)
            act.wait_ge(s_gm2, 1)
            root(pair[0])
            with act.Fori(0, B) as b:
                uses = Uses(act, b)

                for what, i, place in ACT_PROLOGUE:
                    home = prologue_home(uses, b, what, i, place)
                    if what == "s":
                        act.wait_ge(s_max, b * (NG * NQ * NT) + i + 1)
                        exp0(home, i, nm_first[:, i:i + 1], z_first[:, i:i + 1], p0[0][:, i, :])
                        continue
                    act.wait_ge(home.s_full, home.filled)
                    if what == "q":
                        act.activation(qh, home.bank[:, 0:N], ACT.Identity, bias=qb).then_inc(s_qhi, 1)
                    else:
                        dst, bias = (kh, kb) if what == "k" else (vh, zero)
                        act.activation(dst[:, i * QW:(i + 1) * QW], home.bank[:, :], ACT.Identity,
                                       bias=bias).then_inc(s_ph, 1)
                with act.Fori(0, NG - 1) as g:
                    group_0(b, g, False)
                group_0(b, NG - 1, True)

                phi_hi(b, 1)
                phi_hi(b, 2)
                iteration_1(b, -1, False, True)
                with act.Fori(0, NG - 1) as g:
                    iteration_1(b, g, True, True)
                iteration_1(b, NG - 1, True, False)
                wait_full(act, uses, U_STATS)
                root(slot[U_STATS % 2])

        @block.vector
        def _(dve):
            def minus(dst, src, bias, high):
                return dve.scalar_tensor_tensor(out=dst, in0=src, scalar=bias, in1=high.bitcast(F32),
                                                op0=ALU.add, op1=ALU.subtract)

            dve.memset(zero, 0.0)
            dve.memset(eps, EPS)
            dve.memset(xr[:, L:L + N], 0.0).then_inc(s_const, 1)
            dve.wait_ge(s_const, 4)
            rows = 2 * WROW
            dve.tensor_tensor(pick_both[0:rows, :], ident[0:rows, 0:NQ * NT], ident[0:rows, WROW:WROW + NQ * NT],
                              ALU.add).then_inc(s_pick, 1)
            dve.memset(w2[:, :], 0.0)
            dve.wait_ge(s_pick, 1)
            both = pick_both[0:rows, :].rearrange("p (q t) -> p q t", q=NQ)
            dve.tensor_reduce(pick_tile[0:rows, :], both.rearrange("p q t -> p t q"), AXX, ALU.add)
            dve.tensor_reduce(pick_q[0:rows, :], both, AXX, ALU.add).then_inc(s_pick, 1)
            dve.wait_ge(s_pick, 2)
            dve.tensor_copy(pick_quarter[0:rows, :], pick_q[0:rows, :])

            def softmax_weights(i, nm, z, nmn, df, e, ezt, zs, zr, wt, s):
                s_mn_, s_df_, s_e_, s_ez_, s_zs_, s_zr_, s_w_ = s
                if df is not None:
                    dve.tensor_reduce(nmn, tq(nm), AXX, ALU.min).then_inc(s_mn_, 1)
                    dve.wait_ge(s_mn_, i(1, 1))
                    dve.tensor_tensor(qt(df), nmn.unsqueeze(1).broadcast_to([P, NQ, NT]), nm,
                                      ALU.subtract).then_inc(s_df_, 1)
                if e is not None:
                    dve.wait_ge(s_e_, i(1, 1))
                    dve.tensor_tensor(qt(ezt), qt(e), z, ALU.mult).then_inc(s_ez_, 1)
                    dve.wait_ge(s_ez_, i(1, 1))
                    dve.tensor_reduce(zs, tq(qt(ezt)), AXX, ALU.add).then_inc(s_zs_, 1)
                    dve.wait_ge(s_zs_, i(1, 1))
                    dve.reciprocal(zr, zs).then_inc(s_zr_, 1)
                    dve.wait_ge(s_zr_, i(1, 1))
                    for at in (0, WROW):
                        ins = dve.tensor_tensor(qt(wt[:, at:at + NQ * NT]), qt(e),
                                                zr.unsqueeze(1).broadcast_to([P, NQ, NT]), ALU.mult)
                    ins.then_inc(s_w_, 1)

            def phi_lo(b, c):
                u, cols = phi_use(c), slice(c * QW, (c + 1) * QW)
                dve.wait_ge(s_phi, b * NQ + c + 1)
                minus(phl[:, cols], slot[u % 2][:, :], bph, phh[:, cols]).then_inc(s_free[u % 2], 1)

            def maximum_1(home, n):
                q, t = n // NT, n % NT
                dve.wait_ge(home.s_full, home.filled)
                dve.tensor_reduce(nm1[:, q, t:t + 1], home.bank[:, :], AXX, ALU.max, negate=True).then_inc(s_max1, 1)

            def group_0(b, g, last):
                uses = Uses(dve, b, g, PER_G0)
                gi = Groups(dve, b, g, NG)
                chain = (s_mn, s_df, s_e, s_ez, s_zs, s_zr, s_w)

                def lo(n):
                    dve.wait_ge(s_hi, gi(NM, n + 1))
                    dve.tensor_tensor(ptl[n % PT_RING], t_bank[n % 2], pth[n % PT_RING].bitcast(F32),
                                      ALU.subtract).then_inc(s_lo[n % 2], 1)

                for n in range(NM):
                    q, j = n // MT, n % MT
                    lo(n)
                    if n == W_STEP:
                        u = U_G0 + w_use(0, last)
                        dve.wait_ge(s_wh, gi(1, 1))
                        dve.tensor_tensor(wt2[WROW:, :], slot[u % 2][WROW:2 * WROW, 0:P],
                                          wt2[WROW:, :].bitcast(F32), ALU.subtract).then_inc(s_free[u % 2], 1)
                    if q == NQ - 2 and j == 6 and not last:
                        dve.wait_ge(s_qhi, gi(1, 2))
                        u = U_G0 + U_QPROJ
                        minus(ql, slot[u % 2][:, 0:N], qb, qh).then_inc(s_free[u % 2], 1)
                    if last and (q, j) in FIRST_1:
                        t = FIRST_1[q, j]
                        if t == "phi":
                            phi_lo(b, 0)
                        elif t == "theta":
                            dve.wait_ge(s_thh, b * (NG + 1) + 1)
                            minus(th[CI:P, :], slot[U_TH0 % 2][CI:P, 0:N], bth[CI:P, :], th[CI:P, :]).then_inc(
                                s_free[U_TH0 % 2], 1)
                        else:
                            maximum_1(score_home(Uses(dve, b, -1, PER_G1), b, t, True), t)
                    if j in SCORES_AT[q] and not (last and q == NQ - 1):
                        t = SCORES_AT[q][j]
                        u = U_G0 + score_use_0(q, t)
                        wait_full(dve, uses, u)
                        dst = nm_first[:, t:t + 1] if q == NQ - 1 else nmg[:, q + 1, t:t + 1]
                        dve.tensor_reduce(dst, slot[u % 2][:, :], AXX, ALU.max, negate=True).then_inc(s_max, 1)
                    if q == 0 and j == 1:
                        for u in PREV_LAST:
                            wait_given_up(dve, uses, u)
                        dve.tensor_copy(nmg[:, 0, :], nm_first).then_inc(s_cp, 1)
                        dve.tensor_copy(zg[:, 0, :], z_first).then_inc(s_cp, 1)
                    if q == NQ - 1 and j == 0:
                        u = U_G0 + score_use_0(NQ - 2, NT - 1)
                        wait_given_up(dve, uses, u - 1)
                        wait_given_up(dve, uses, u)
                        dve.wait_ge(s_cp, gi(2, 2))
                        softmax_weights(gi, nmg, zg, nmin, diff, None, None, None, None, None, chain)
                    if q == NQ - 1 and j == 2:
                        softmax_weights(gi, None, zg, None, None, efac, ez, zsum, zrec, w2, chain)

            def iteration_1(b, g, has_pv, has_scores):
                first_run = not has_pv
                uses = Uses(dve, b, g, PER_G1)
                gi, gth = Groups(dve, b, g, NG), Groups(dve, b, g, NG + 1)

                nxt = Groups(dve, b, g + 1, NG)

                def add_sum(q):
                    m = q * NS + NS - 1
                    dve.wait_ge(s_pvs[m % HL_RING], gi(NQ * NS // HL_RING, CREDIT + m // HL_RING + 1))
                    dve.wait_ge(s_acc[q % 2], gi(2, CREDIT + q // 2))
                    dve.tensor_tensor(acc[:, q * QW:(q + 1) * QW], pair[q % 2][:, :], acc[:, q * QW:(q + 1) * QW],
                                      ALU.add).then_inc(s_acc[q % 2], 1)

                def lo(n):
                    q, t = n // NT, n % NT
                    m = q * NS + SPLIT.index(t)
                    dve.wait_ge(s_hi1, gi(NQ * NS, m + 1))
                    dve.tensor_tensor(hll[m % HL_RING], f[:, q % NQ, t, :], hlh[m % HL_RING].bitcast(F32),
                                      ALU.subtract).then_inc(s_lo1, 1)

                def theta_lo():
                    u = use_1("theta", first_run)
                    dve.wait_ge(s_thh, gth(1, 3))
                    minus(tn[CI:P, :], slot[u % 2][CI:P, 0:N], bth[CI:P, :], tn[CI:P, :]).then_inc(s_free[u % 2], 1)

                def g_rows():
                    u = use_1("g", first_run)
                    wait_full(dve, uses, u)
                    if has_pv:
                        dve.wait_ge(s_g, gi(NQ * NS, NQ * NS))
                    dve.tensor_tensor(gsb[:, :].rearrange("p (t c) -> p t c", t=NT),
                                      slot[u % 2][:, 0:NT * CI].rearrange("p (t c) -> p t c", t=NT),
                                      gbb[:, :].unsqueeze(1).broadcast_to([P, NT, CI]),
                                      ALU.add).then_inc(s_free[u % 2], 1)

                def offsets(h):
                    c = HALVES[h]
                    dve.wait_ge(s_max1, gi(NQ * NT, NQ * NT + (NQ - 1) * NT + c.stop))
                    dve.tensor_reduce(nmin1[:, c], nm1[:, :, c].rearrange("p q t -> p t q"), AXX, ALU.min).then_inc(
                        s_mn1[h], 1)
                    dve.wait_ge(s_mn1[h], nxt(1, 1))
                    dve.tensor_tensor(diff1[:, :, c], nmin1[:, c].unsqueeze(1).broadcast_to([P, NQ, 2]), nm1[:, :, c],
                                      ALU.subtract).then_inc(s_df1[h], 1)

                def row_sums(h):
                    c = HALVES[h]
                    for t in range(c.start, c.stop):
                        home = score_home(uses, b, (NQ - 1) * NT + t, first_run)
                        dve.wait_ge(home.s_free, home.given_up)
                    dve.wait_ge(s_e1[h], nxt(1, 1))
                    dve.tensor_tensor(ez1[:, :, c], efac1[:, :, c], z1[:, :, c], ALU.mult).then_inc(s_ez1[h], 1)
                    dve.wait_ge(s_ez1[h], nxt(1, 1))
                    dve.tensor_reduce(zsum1[:, c], ez1[:, :, c].rearrange("p q t -> p t q"), AXX, ALU.add).then_inc(
                        s_zs1[h], 1)

                def weights_1(h):
                    c = HALVES[h]
                    dve.wait_ge(s_zs1[h], nxt(1, 1))
                    dve.reciprocal(zrec1[:, c], zsum1[:, c]).then_inc(s_zr1[h], 1)
                    dve.wait_ge(s_zr1[h], nxt(1, 1))
                    dve.tensor_tensor(wgt1[:, :, c], efac1[:, :, c], zrec1[:, c].unsqueeze(1).broadcast_to([P, NQ, 2]),
                                      ALU.mult).then_inc(s_w1[h], 1)

                for q in range(1 if first_run else 0, NQ):
                    if first_run and q == NQ - 2:
                        phi_lo(b, NQ - 1)
                    for what in DVE_ORDER[q]:
                        kind, i = what[0], q * NT + int(what[1])
                        if kind == "L" and (has_pv if i < NQ * NT else has_scores):
                            lo(i)
                        if kind == "M" and has_scores:
                            maximum_1(score_home(uses, b, i, first_run), i)
                        if kind == "A" and has_pv:
                            add_sum(int(what[1]))
                            if not has_scores and int(what[1]) > 0:
                                final_sum(b, int(what[1]) - 1)
                            if not has_scores and int(what[1]) == NQ - 2:
                                offset_moment(b + 1, slot[U_STATS % 2])
                        if kind == "T" and has_scores:
                            theta_lo()
                        if kind == "G" and has_scores:
                            g_rows()
                        if has_scores and kind in "DRW":
                            {"D": offsets, "R": row_sums, "W": weights_1}[kind](int(what[1]))
                    if not has_scores and q == NQ - 2:
                        for c in range(NG):
                            chunk_stats(b + 1, c)
                        channel_stats(b + 1)

            def chunk_stats(b, c):
                if c % 2 == 0:
                    dve.wait_ge(s_x[c // 2], b * 16 + 16)
                dve.bn_stats(bst[:, c, :], xc[:, c * N:(c + 1) * N]).then_inc(s_bs, 1)

            def channel_stats(b):
                dve.wait_ge(s_bs, b * NG + NG)
                dve.memset(gn[:, 6:7], 0.0)
                dve.bn_aggr(mv[:, :], bst[:, :, :]).then_inc(s_mv, 1)

            def offset_moment(b, bank):
                dve.wait_ge(s_gm, b + 1)
                dve.wait_ge(s_mv, b + 1)
                dve.tensor_tensor(dmean, mv[:, 0:1], bank[:, 0:1], ALU.subtract).then_inc(s_dm, 1)
                dve.wait_ge(s_dm, b + 1)
                dve.scalar_tensor_tensor(out=e2, in0=dmean, scalar=dmean, in1=mv[:, 1:2], op0=ALU.mult,
                                         op1=ALU.add).then_inc(s_e2, 1)

            def gains(b, bank, done):
                dve.wait_ge(s_std, b + 1)
                dve.reciprocal(rstd, std).then_inc(s_rstd, 1)
                dve.tensor_copy(gmean, bank[:, 0:1]).then_inc(done, 1)
                dve.wait_ge(s_rstd, b + 1)
                dve.tensor_tensor(gain, rstd, gamma, ALU.mult).then_inc(s_gain, 1)

            def normalise(b, c):
                dve.wait_ge(s_gain, b + 1)
                cols = xc[:, c * QW:(c + 1) * QW]
                dve.tensor_scalar(cols, cols, gmean, gain, ALU.subtract, ALU.mult).then_inc(s_xn, 1)

            def final_sum(b, c):
                uses = Uses(dve, b)
                u = out_use(c)
                wait_full(dve, uses, u)
                cols = xr[:, c * QW:(c + 1) * QW]
                dve.scalar_tensor_tensor(out=cols, in0=slot[u % 2][:, :], scalar=bout, in1=cols,
                                         op0=ALU.add, op1=ALU.add).then_inc(s_free[u % 2], 1)

            for c in range(NG):
                chunk_stats(0, c)
            channel_stats(0)
            dve.wait_ge(s_wl, 16 * len(w))
            dve.tensor_scalar(wqs[:, :], wq[:, :], SCALE, None, ALU.mult)
            dve.wait_ge(s_setup_pe, 1)
            dve.tensor_copy(wvo[:, :], pair[0][:, 0:P]).then_inc(s_setup, 1)
            dve.tensor_scalar(qb, pair[1][:, 0:1], bq, SCALE, ALU.add, ALU.mult)
            dve.tensor_tensor(kb, pair[1][:, 1:2], bk, ALU.add)
            dve.tensor_copy(gbb[:, :], pair[1][:, 2:2 + CI])
            dve.wait_ge(s_setup_pe, 2)
            dve.tensor_tensor(vb, pair[0][:, N:N + 1], bo, ALU.add).then_inc(s_setup, 1)
            dve.wait_ge(s_setup, 2)
            offset_moment(0, pair[0])
            gains(0, pair[0], s_gmc)
            dve.wait_ge(s_gmc, 1)
            for c in range(NQ):
                normalise(0, c)
            with dve.Fori(0, B) as b:
                uses = Uses(dve, b)
                for what, i, place in PROLOGUE:
                    home = prologue_home(uses, b, what, i, place)
                    if what == "s":
                        dve.wait_ge(home.s_full, home.filled)
                        dve.tensor_reduce(nm_first[:, i:i + 1], home.bank[:, :], AXX, ALU.max,
                                          negate=True).then_inc(s_max, 1)
                    elif what == "q":
                        dve.wait_ge(s_qhi, b * NG + 1)
                        minus(ql, home.bank[:, 0:N], qb, qh).then_inc(home.s_free, 1)
                    else:
                        high, low, bias = (kh, kl, kb) if what == "k" else (vh, vl, zero)
                        cols = slice(i * QW, (i + 1) * QW)
                        dve.wait_ge(s_ph, b * (2 * NQ) + (i if what == "k" else NQ + i) + 1)
                        minus(low[:, cols], home.bank[:, :], bias, high[:, cols]).then_inc(home.s_free, 1)
                with dve.Fori(0, NG - 1) as g:
                    group_0(b, g, False)
                group_0(b, NG - 1, True)

                phi_lo(b, 1)
                phi_lo(b, 2)
                dve.wait_ge(s_az, b + 1)
                iteration_1(b, -1, False, True)
                with dve.Fori(0, NG - 1) as g:
                    iteration_1(b, g, True, True)
                iteration_1(b, NG - 1, True, False)
                gains(b + 1, slot[U_STATS % 2], s_free[U_STATS % 2])
                wait_given_up(dve, uses, U_STATS)
                normalise(b + 1, 0)
                normalise(b + 1, 1)
                final_sum(b, NQ - 1)
                normalise(b + 1, 2)
                normalise(b + 1, 3)

        @block.gpsimd
        def _(pool):
            pool.memset(ident[:, :], 0.0).then_inc(s_const, 1)
            pool.memset(gmat[:, :], 1.0 / GROUP_CHANNELS)
            pool.memset(ones[:, :], 1.0)
            pool.memset(zeros[:, :], 0.0)
            for i in range(2):
                pool.memset(gwh[i][:, :, :], 0.0)
            blocks = gmat[:, :].rearrange("p (a c) -> p a c", c=GROUP_CHANNELS)
            pool.drain().then_inc(s_const, 1)
            pool.wait_ge(s_const, 3)
            pool.affine_select(out=ident[:, :], in_=ident[:, :], compare_op=ALU.not_equal, fill=1.0, base=0,
                               pattern=[[-1, P]], channel_multiplier=1)
            pool.affine_select(out=blocks, in_=blocks, compare_op=ALU.is_ge, fill=0.0, base=0,
                               pattern=[[-GROUP_CHANNELS, P // GROUP_CHANNELS], [0, GROUP_CHANNELS]],
                               channel_multiplier=1).then_inc(s_masks, 1)
            pool.wait_ge(s_masks, 1)
            pool.affine_select(out=blocks, in_=blocks, compare_op=ALU.is_ge, fill=0.0, base=GROUP_CHANNELS - 1,
                               pattern=[[GROUP_CHANNELS, P // GROUP_CHANNELS], [0, GROUP_CHANNELS]],
                               channel_multiplier=-1).then_inc(s_const, 1)

            def group_0(b, g, last):
                uses = Uses(pool, b, g, PER_G0)
                gi = Groups(pool, b, g, NG)
                wait_given_up(pool, uses, U_G0 + w_use(0, last))
                pool.tensor_tensor(wspread[:, :].rearrange("p (t n) -> p t n", t=NT),
                                   wt2[:, :].bitcast(F32).unsqueeze(1).broadcast_to([2 * WROW, NT, P]),
                                   pick_tile[0:2 * WROW, :].unsqueeze(2).broadcast_to([2 * WROW, NT, P]),
                                   ALU.mult).then_inc(s_wx, 1)
                for j in (1, 2):
                    wait_given_up(pool, uses, U_G0 + w_use(j, last))
                for i in range(2):
                    pool.wait_ge(s_oev[i], gi(2, CREDIT + 2))
                pool.tensor_tensor(osb, osb, wb, ALU.mult).then_inc(s_pr, 1)
                pool.wait_ge(s_pr, gi(1, CREDIT + 1))
                pool.tensor_tensor(wb[:, 0:QW], osb[:, 0:QW], osb[:, QW:2 * QW], ALU.add).then_inc(s_h1, 1)
                pool.wait_ge(s_h1, gi(1, CREDIT + 1))
                pool.tensor_tensor(xs[:, :], wb[:, 0:N], wb[:, N:2 * N], ALU.add).then_inc(s_h2, 1)
                pool.wait_ge(s_xb, b + 1)
                pool.wait_ge(s_h2, gi(1, CREDIT + 1))
                cols = xr[:, bass.ts(g, N)] if not last else xr[:, g * N:(g + 1) * N]
                pool.tensor_tensor(cols, cols, xs[:, :], ALU.add).then_inc(s_x1, 1)

            def iteration_1(b, g, has_pv, has_scores):
                first_run = not has_pv
                uses = Uses(pool, b, g, PER_G1)
                gi = Groups(pool, b, g, NG)
                rows = gsb[:, :].rearrange("p (t c) -> p t c", t=NT)
                part = gtmp[:, :].rearrange("p (t c) -> p t c", t=NS)
                for q in range(NQ):
                    if has_pv:
                        pool.wait_ge(s_acc[q % 2], gi(2, CREDIT + q // 2))
                        for t in range(NT):
                            if q == 0 and t in (HALVES[0].start, HALVES[1].start):
                                pool.wait_ge(s_w1[t // HALVES[1].start], gi(1, 1))
                            g_rows, weight = rows[:, t, :], wgt1[:, q, t:t + 1].broadcast_to([P, CI])
                            if t in WHOLE:
                                pool.tensor_tensor(gwh[q % 2][:, WHOLE.index(t), 0:CI], g_rows, weight,
                                                   ALU.mult).then_inc(s_gw, 1)
                                continue
                            i = SPLIT.index(t)
                            m = q * NS + i
                            hi_half, both = ghl[q % 2][:, i, 0:CI], part[:, i, :]
                            pool.tensor_tensor(both, g_rows, weight, ALU.mult).then_inc(s_gt, 1)
                            pool.wait_ge(s_gt, gi(NQ * NS, m + 1))
                            pool_copy(hi_half, both, zeros[:, 0:CI]).then_inc(s_gh, 1)
                            pool.wait_ge(s_gh, gi(NQ * NS, m + 1))
                            pool.tensor_tensor(ghl[q % 2][:, i, CI:P], both, hi_half.bitcast(F32),
                                               ALU.subtract).then_inc(s_g, 1)
                        pool.wait_ge(s_g, gi(NQ * NS, q * NS + NS))
                    if has_scores and q == 1:
                        if has_pv:
                            wait_given_up(pool, uses, use_1("g", False) - PER_G1)
                        else:
                            pool.wait_ge(s_x1, b * NG + NG)
                        pool_copy(xs[:, :], xr[:, bass.ds(g * N + N, N)], zeros[:, :]).then_inc(s_xs, 1)
                    if has_scores and q == NQ - 1:
                        wait_given_up(pool, uses, use_1("theta", first_run))
                        for t in range(NT):
                            home = score_home(uses, b, q * NT + t, first_run)
                            pool.wait_ge(home.s_full, home.filled)
                            pool_copy(th[:, t * P:(t + 1) * P], tn[:, t * P:(t + 1) * P].bitcast(F32),
                                      zeros[:, 0:P]).then_inc(s_th, 1)

            pool.wait_ge(s_setup, 2)
            with pool.Fori(0, B) as b:
                pool.wait_ge(s_xr, b * 16 + 16)
                pool.tensor_tensor(xr[:, 0:L], xr[:, 0:L], vb.broadcast_to([P, L]), ALU.add).then_inc(s_xb, 1)
                with pool.Fori(0, NG - 1) as g:
                    group_0(b, g, False)
                zeros8 = zeros[:, :].unsqueeze(1).broadcast_to([P, NG, N])
                pool_copy(acc[:, :].rearrange("p (a n) -> p a n", a=NG), zeros8, zeros8).then_inc(s_az, 1)
                group_0(b, NG - 1, True)
                iteration_1(b, -1, False, True)
                with pool.Fori(0, NG - 1) as g:
                    iteration_1(b, g, True, True)
                iteration_1(b, NG - 1, True, False)


def kernel(**inputs):
    import numpy as np
    import concourse.bacc as bacc
    from concourse.bass_utils import run_bass_kernel_spmd as run

    nc = bacc.Bacc("TRN2", target_bir_lowering=False, num_devices=1)
    arrays = {}

    def given(name, a):
        a = np.ascontiguousarray(a)
        arrays[name] = a
        return nc.dram_tensor(name, a.shape, F32, kind="ExternalInput").ap()

    def col(a):
        return np.asarray(a).reshape(-1, 1)

    x = given("in_x", np.asarray(inputs["x"]).reshape(B, P, L))
    i0 = {k[len("L0_conv_"):]: np.asarray(v) for k, v in inputs.items() if k.startswith("L0_conv_")}
    i1 = {k[len("L1_conv_"):]: np.asarray(v) for k, v in inputs.items() if k.startswith("L1_conv_")}
    wth, bth = given("theta_w_t", i1["theta_w"].T), given("theta_b", col(i1["theta_b"]))
    wph, bph = given("phi_w_t", i1["phi_w"].T), given("phi_b", col(i1["phi_b"]))
    wout = given("W_w_t", i1["W_w"].T)
    w = [
        ("wq", given("wq_t", i0["wq"].T)), ("wk", given("wk_t", i0["wk"].T)), ("wv", given("wv", i0["wv"])),
        ("wo", given("wo_t", i0["wo"].T)), ("wg", given("g_w_t", i1["g_w"].T)),
        ("gbrow", given("g_b", i1["g_b"].reshape(1, -1))),
        ("gamma", given("gamma", col(i0["gamma"]))), ("beta", given("beta", col(i0["beta"]))),
        ("bq", given("bq", col(i0["bq"]))), ("bk", given("bk", col(i0["bk"]))),
        ("bv", given("bv", col(i0["bv"]))), ("bo", given("bo", col(i0["bo"]))),
        ("bout", given("W_b", col(i1["W_b"]))),
        ("wth0", wth), ("wth1", wth), ("wph0", wph), ("wph1", wph), ("wout0", wout), ("wout1", wout),
        ("bth0", bth), ("bth1", bth), ("bph0", bph), ("bph1", bph),
    ]
    out = nc.dram_tensor("out_0", (B, P, 64, 64), F32, kind="ExternalOutput").ap()
    build(nc, x, out.rearrange("b c h w -> b c (h w)"), w)
    r = run(nc, [arrays], core_ids=[0])
    return r.results[0]["out_0"]
```
